# Optimizing a Trainium2 kernel written in Bass

```python
import numpy as np
import jax
import jax.numpy as jnp

def _softmax(x, axis=-1):
    return jax.nn.softmax(x, axis=axis)

def _gelu(x):
    return jax.nn.gelu(x, approximate=True)

def _silu(x):
    return jax.nn.silu(x)

def _sigmoid(x):
    return jax.nn.sigmoid(x)

def _layernorm(x, axis=-1, eps=1e-05):
    m = jnp.mean(x, axis=axis, keepdims=True)
    v = jnp.var(x, axis=axis, keepdims=True)
    return (x - m) / jnp.sqrt(v + eps)

def _scatter_add(tgt, idx, src, axis=0):
    return tgt.at[idx].add(src)

def _segment_sum(src, seg, n):
    return jax.ops.segment_sum(src, seg, n)
kernel_name = 'mk_audio_tower_d1_tok_audfeat256_r4_b3420e'

def setup_inputs(seed: int=0):
    np.random.seed(seed)
    _w = jnp.asarray

    def _rec_inputs():
        import jax
        import jax.numpy as jnp
        _rk = jax.random.key(seed)
        x = 7.22013e-05 + 1.00017 * jax.random.normal(jax.random.fold_in(_rk, 1), (64, 256, 128), jnp.float32)
        return x
    x = _rec_inputs()

    def _L0_tok_setup():
        import jax, jax.numpy as jnp
        import numpy as np
        FILTER_SIZE = 8
        INPUT_DIM = 128
        KERNEL_SIZE = 64
        key = jax.random.key(seed)
        k1, k2, k3, k4 = jax.random.split(key, 4)
        user_batch = jax.random.normal(k1, (32, 512, INPUT_DIM), dtype=jnp.float32)
        filt = jax.random.uniform(k2, (FILTER_SIZE, INPUT_DIM), dtype=jnp.float32)
        W_k = jax.random.uniform(k3, (FILTER_SIZE * INPUT_DIM, KERNEL_SIZE), dtype=jnp.float32)
        b_k = jax.random.uniform(k4, (KERNEL_SIZE,), dtype=jnp.float32)
        return {'user_batch': user_batch, 'filt': filt, 'W_k': W_k, 'b_k': b_k}
    _L0_tok_all = _L0_tok_setup()
    _L0_tok_in = {k: v for k, v in _L0_tok_all.items() if k in ('filt', 'W_k', 'b_k')}
    del _L0_tok_all

    def _L0_attn_setup():
        import jax, jax.numpy as jnp
        import numpy as np
        B, T, D = (4, 512, 64)
        W_LORA, A_LORA, G_LORA = (64, 64, 128)
        DECAY_SCALE = -0.6065306597126334
        EPS = D * 1e-05

        def _forward(x, x_mix, W_r, W_k, W_v, W_o, A_w, B_w, b_w, A_a, B_a, b_a, A_g, B_g, k_k, k_a, r_k, gn_w, gn_b):
            b, t, d = x.shape
            shifted = jnp.pad(x, ((0, 0), (1, 0), (0, 0)))[:, :-1]
            delta = shifted - x
            xr, xw, xk, xv, xa, xg = [x + delta * x_mix[i] for i in range(6)]
            r = xr @ W_r
            w = DECAY_SCALE * jax.nn.sigmoid(jnp.tanh(xw @ A_w) @ B_w + b_w)
            k = xk @ W_k
            v = xv @ W_v
            a = jax.nn.sigmoid(xa @ A_a @ B_a + b_a)
            g = jax.nn.sigmoid(xg @ A_g) @ B_g
            kk = k * k_k
            kk = kk / jnp.maximum(jnp.linalg.norm(kk, axis=-1, keepdims=True), 1e-12)
            k = k * (1.0 + (a - 1.0) * k_a)
            decay = jnp.exp(w)

            def step(S, inp):
                r_t, dec_t, k_t, v_t, kk_t, a_t = inp
                b_t = kk_t * a_t
                sa = jnp.einsum('bvk,bk->bv', S, -kk_t)
                S = S * dec_t[:, None, :] + sa[:, :, None] * b_t[:, None, :] + v_t[:, :, None] * k_t[:, None, :]
                o_t = jnp.einsum('bvk,bk->bv', S, r_t)
                return (S, o_t)
            tm = lambda z: jnp.swapaxes(z, 0, 1)
            S0 = jnp.zeros((b, d, d), x.dtype)
            _, o = jax.lax.scan(step, S0, (tm(r), tm(decay), tm(k), tm(v), tm(kk), tm(a)))
            o = jnp.swapaxes(o, 0, 1)
            mu = jnp.mean(o, axis=-1, keepdims=True)
            var = jnp.var(o, axis=-1, keepdims=True)
            o = (o - mu) * jax.lax.rsqrt(var + EPS) * gn_w + gn_b
            o = o + jnp.sum(r * k * r_k, axis=-1, keepdims=True) * v
            return o * g @ W_o
        key = jax.random.key(seed)
        ks = jax.random.split(key, 20)
        n = jax.random.normal
        p = {}
        p['x'] = n(ks[0], (B, T, D), jnp.float32)
        p['x_mix'] = n(ks[1], (6, D), jnp.float32) * 0.1
        s = 1.0 / np.sqrt(D).astype(np.float32)
        p['W_r'] = n(ks[2], (D, D), jnp.float32) * s
        p['W_k'] = n(ks[3], (D, D), jnp.float32) * s
        p['W_v'] = n(ks[4], (D, D), jnp.float32) * s
        p['W_o'] = n(ks[5], (D, D), jnp.float32) * s
        p['A_w'] = n(ks[6], (D, W_LORA), jnp.float32) * s
        p['B_w'] = n(ks[7], (W_LORA, D), jnp.float32) / np.sqrt(W_LORA).astype(np.float32)
        p['b_w'] = n(ks[8], (D,), jnp.float32) * 0.5
        p['A_a'] = n(ks[9], (D, A_LORA), jnp.float32) * s
        p['B_a'] = n(ks[10], (A_LORA, D), jnp.float32) / np.sqrt(A_LORA).astype(np.float32)
        p['b_a'] = n(ks[11], (D,), jnp.float32) * 0.1
        p['A_g'] = n(ks[12], (D, G_LORA), jnp.float32) * s
        p['B_g'] = n(ks[13], (G_LORA, D), jnp.float32) / np.sqrt(G_LORA).astype(np.float32)
        p['k_k'] = n(ks[14], (D,), jnp.float32) * 0.5 + 0.85
        p['k_a'] = n(ks[15], (D,), jnp.float32) * 0.1 + 1.0
        p['r_k'] = n(ks[16], (D,), jnp.float32) * 0.1
        p['gn_w'] = jnp.ones((D,), jnp.float32)
        p['gn_b'] = jnp.zeros((D,), jnp.float32)
        return p
    _L0_attn_all = _L0_attn_setup()
    _L0_attn_in = {k: v for k, v in _L0_attn_all.items() if k in ('x_mix', 'W_r', 'W_k', 'W_v', 'W_o', 'A_w', 'B_w', 'b_w', 'A_a', 'B_a', 'b_a', 'A_g', 'B_g', 'k_k', 'k_a', 'r_k', 'gn_w', 'gn_b')}
    del _L0_attn_all

    def _L0_ffn_setup():
        import jax, jax.numpy as jnp
        import numpy as np
        E = 8
        K = 2
        D = 64
        H = 128
        DOUT = 64
        EPS = 1e-05
        key = jax.random.key(seed)
        ks = jax.random.split(key, 9)
        s = 0.02
        return {'x': jax.random.normal(ks[0], (4, 2048, D), jnp.float32), 'gamma': 1.0 + 0.05 * jax.random.normal(ks[1], (D,), jnp.float32), 'beta': 0.05 * jax.random.normal(ks[2], (D,), jnp.float32), 'Wr': 0.01 * jax.random.normal(ks[3], (D, E), jnp.float32), 'br': jnp.zeros((E,), jnp.float32), 'W1': s * jax.random.normal(ks[4], (E, D, H), jnp.float32), 'b1': s * jax.random.normal(ks[5], (E, H), jnp.float32), 'W2': s * jax.random.normal(ks[6], (E, H, DOUT), jnp.float32), 'b2': s * jax.random.normal(ks[7], (E, DOUT), jnp.float32)}
    _L0_ffn_all = _L0_ffn_setup()
    _L0_ffn_in = {k: v for k, v in _L0_ffn_all.items() if k in ('gamma', 'beta', 'Wr', 'br', 'W1', 'b1', 'W2', 'b2')}
    del _L0_ffn_all
    return {'x': x, 'L0_tok_filt': _L0_tok_in['filt'], 'L0_tok_W_k': _L0_tok_in['W_k'], 'L0_tok_b_k': _L0_tok_in['b_k'], 'L0_attn_x_mix': _L0_attn_in['x_mix'], 'L0_attn_W_r': _L0_attn_in['W_r'], 'L0_attn_W_k': _L0_attn_in['W_k'], 'L0_attn_W_v': _L0_attn_in['W_v'], 'L0_attn_W_o': _L0_attn_in['W_o'], 'L0_attn_A_w': _L0_attn_in['A_w'], 'L0_attn_B_w': _L0_attn_in['B_w'], 'L0_attn_b_w': _L0_attn_in['b_w'], 'L0_attn_A_a': _L0_attn_in['A_a'], 'L0_attn_B_a': _L0_attn_in['B_a'], 'L0_attn_b_a': _L0_attn_in['b_a'], 'L0_attn_A_g': _L0_attn_in['A_g'], 'L0_attn_B_g': _L0_attn_in['B_g'], 'L0_attn_k_k': _L0_attn_in['k_k'], 'L0_attn_k_a': _L0_attn_in['k_a'], 'L0_attn_r_k': _L0_attn_in['r_k'], 'L0_attn_gn_w': _L0_attn_in['gn_w'], 'L0_attn_gn_b': _L0_attn_in['gn_b'], 'L0_ffn_gamma': _L0_ffn_in['gamma'], 'L0_ffn_beta': _L0_ffn_in['beta'], 'L0_ffn_Wr': _L0_ffn_in['Wr'], 'L0_ffn_br': _L0_ffn_in['br'], 'L0_ffn_W1': _L0_ffn_in['W1'], 'L0_ffn_b1': _L0_ffn_in['b1'], 'L0_ffn_W2': _L0_ffn_in['W2'], 'L0_ffn_b2': _L0_ffn_in['b2']}

def reference(x, L0_tok_filt, L0_tok_W_k, L0_tok_b_k, L0_attn_x_mix, L0_attn_W_r, L0_attn_W_k, L0_attn_W_v, L0_attn_W_o, L0_attn_A_w, L0_attn_B_w, L0_attn_b_w, L0_attn_A_a, L0_attn_B_a, L0_attn_b_a, L0_attn_A_g, L0_attn_B_g, L0_attn_k_k, L0_attn_k_a, L0_attn_r_k, L0_attn_gn_w, L0_attn_gn_b, L0_ffn_gamma, L0_ffn_beta, L0_ffn_Wr, L0_ffn_br, L0_ffn_W1, L0_ffn_b1, L0_ffn_W2, L0_ffn_b2):
    import jax
    import jax.numpy as jnp

    def _L0_tok_ref(user_batch, filt, W_k, b_k):
        import jax, jax.numpy as jnp
        import numpy as np
        FILTER_SIZE = 8
        INPUT_DIM = 128
        KERNEL_SIZE = 64
        B, L, D = user_batch.shape
        F = filt.shape[0]
        n_win = L - F
        idx = jnp.arange(n_win)[:, None] + jnp.arange(F)[None, :]
        windows = user_batch[:, idx, :]
        W = W_k.reshape(F, D, -1)
        out = jnp.einsum('blfd,fd,fdk->blk', windows, filt, W)
        return jax.nn.relu(out + b_k)

    def _L0_attn_ref(x, x_mix, W_r, W_k, W_v, W_o, A_w, B_w, b_w, A_a, B_a, b_a, A_g, B_g, k_k, k_a, r_k, gn_w, gn_b):
        import jax, jax.numpy as jnp
        import numpy as np
        B, T, D = (4, 512, 64)
        W_LORA, A_LORA, G_LORA = (64, 64, 128)
        DECAY_SCALE = -0.6065306597126334
        EPS = D * 1e-05

        def _forward(x, x_mix, W_r, W_k, W_v, W_o, A_w, B_w, b_w, A_a, B_a, b_a, A_g, B_g, k_k, k_a, r_k, gn_w, gn_b):
            b, t, d = x.shape
            shifted = jnp.pad(x, ((0, 0), (1, 0), (0, 0)))[:, :-1]
            delta = shifted - x
            xr, xw, xk, xv, xa, xg = [x + delta * x_mix[i] for i in range(6)]
            r = xr @ W_r
            w = DECAY_SCALE * jax.nn.sigmoid(jnp.tanh(xw @ A_w) @ B_w + b_w)
            k = xk @ W_k
            v = xv @ W_v
            a = jax.nn.sigmoid(xa @ A_a @ B_a + b_a)
            g = jax.nn.sigmoid(xg @ A_g) @ B_g
            kk = k * k_k
            kk = kk / jnp.maximum(jnp.linalg.norm(kk, axis=-1, keepdims=True), 1e-12)
            k = k * (1.0 + (a - 1.0) * k_a)
            decay = jnp.exp(w)

            def step(S, inp):
                r_t, dec_t, k_t, v_t, kk_t, a_t = inp
                b_t = kk_t * a_t
                sa = jnp.einsum('bvk,bk->bv', S, -kk_t)
                S = S * dec_t[:, None, :] + sa[:, :, None] * b_t[:, None, :] + v_t[:, :, None] * k_t[:, None, :]
                o_t = jnp.einsum('bvk,bk->bv', S, r_t)
                return (S, o_t)
            tm = lambda z: jnp.swapaxes(z, 0, 1)
            S0 = jnp.zeros((b, d, d), x.dtype)
            _, o = jax.lax.scan(step, S0, (tm(r), tm(decay), tm(k), tm(v), tm(kk), tm(a)))
            o = jnp.swapaxes(o, 0, 1)
            mu = jnp.mean(o, axis=-1, keepdims=True)
            var = jnp.var(o, axis=-1, keepdims=True)
            o = (o - mu) * jax.lax.rsqrt(var + EPS) * gn_w + gn_b
            o = o + jnp.sum(r * k * r_k, axis=-1, keepdims=True) * v
            return o * g @ W_o
        return _forward(x, x_mix, W_r, W_k, W_v, W_o, A_w, B_w, b_w, A_a, B_a, b_a, A_g, B_g, k_k, k_a, r_k, gn_w, gn_b)

    def _L0_ffn_ref(x, gamma, beta, Wr, br, W1, b1, W2, b2):
        import jax, jax.numpy as jnp
        import numpy as np
        E = 8
        K = 2
        D = 64
        H = 128
        DOUT = 64
        EPS = 1e-05
        mu = jnp.mean(x, axis=-1, keepdims=True)
        var = jnp.mean(jnp.square(x - mu), axis=-1, keepdims=True)
        xn = (x - mu) * jax.lax.rsqrt(var + EPS) * gamma + beta
        logits = jnp.einsum('bsd,de->bse', xn, Wr) + br
        top_vals, top_idx = jax.lax.top_k(logits, K)
        w = jax.nn.softmax(top_vals, axis=-1)
        w_full = jnp.einsum('bsk,bske->bse', w, jax.nn.one_hot(top_idx, E, dtype=w.dtype))
        y = jnp.zeros(x.shape[:-1] + (DOUT,), x.dtype)
        for e in range(E):
            h = jax.nn.gelu(jnp.einsum('bsd,dh->bsh', xn, W1[e]) + b1[e], approximate=False)
            y_e = jnp.einsum('bsh,hd->bsd', h, W2[e]) + b2[e]
            y = y + y_e * w_full[..., e, None]
        return y
    h = _L0_tok_ref(x, L0_tok_filt, L0_tok_W_k, L0_tok_b_k)
    h = h + _L0_attn_ref(_layernorm(h, axis=-1), L0_attn_x_mix, L0_attn_W_r, L0_attn_W_k, L0_attn_W_v, L0_attn_W_o, L0_attn_A_w, L0_attn_B_w, L0_attn_b_w, L0_attn_A_a, L0_attn_B_a, L0_attn_b_a, L0_attn_A_g, L0_attn_B_g, L0_attn_k_k, L0_attn_k_a, L0_attn_r_k, L0_attn_gn_w, L0_attn_gn_b)
    h = h + _L0_ffn_ref(_layernorm(h, axis=-1), L0_ffn_gamma, L0_ffn_beta, L0_ffn_Wr, L0_ffn_br, L0_ffn_W1, L0_ffn_b1, L0_ffn_W2, L0_ffn_b2)
    return h

_drawn_inputs = setup_inputs


def setup_inputs(seed=0):
    import zlib

    import numpy as np

    out = dict(_drawn_inputs(seed))
    spreads = {'L0_attn_gn_w': (1.0, 0.6), 'L0_attn_gn_b': (0.0, 0.8), 'L0_ffn_br': (0.0, 0.8)}
    factors = {'L0_attn_A_w': 7.88,
     'L0_attn_B_w': 7.846,
     'L0_attn_b_w': 4.068,
     'L0_attn_b_a': 8.0,
     'L0_attn_k_k': 8.0,
     'L0_attn_k_a': 7.611,
     'L0_ffn_gamma': 8.0,
     'L0_ffn_beta': 8.0,
     'L0_ffn_Wr': 8.0,
     'L0_ffn_W1': 8.0,
     'L0_ffn_b1': 34.303,
     'L0_ffn_W2': 8.0,
     'L0_ffn_b2': 45.051}
    for name, (base, spread) in spreads.items():
        noise = np.random.default_rng([zlib.crc32(name.encode()), seed]).standard_normal(out[name].shape)
        drawn = base * np.exp(spread * noise) if base else spread * noise
        out[name] = jnp.asarray(drawn.astype(out[name].dtype))
    for name, factor in factors.items():
        out[name] = (out[name] * factor).astype(out[name].dtype)
    return out
```

```python
from contextlib import ExitStack

import numpy as np

import concourse.bass as bass
from concourse import mybir

F32 = mybir.dt.float32
ALU = mybir.AluOpType
ACT = mybir.ActivationFunctionType
AX_X = mybir.AxisListType.X

P = 128
D = 64
HALF = 64
TAPS = 8
CHUNK = 62
NCH = 4
T = CHUNK * NCH
QUAD = 4
COLS = NCH * P
EXPERTS = 8
HID = 128
LEVELS = 5
DECAY_SCALE = -0.6065306597126334
LN_EPS = 1e-5
GN_EPS = D * 1e-5


PER = dict(
    x_loaded=16, x_turned=1, xT_v=1, xT_s=1, conv_done=1, h_ready=1, h_turned=1, htm_ready=1,
    ln1_sum=1, ln1_mean=1, ln1_cent=1, ln1_sq=1, ln1_ss=1, ln1_var=1, ln1_rstd=1, ln1_done=1,
    x1_turned=1, x1T_ready=1, delta_ready=3, mixed=6,
    lora1_done=4, lora1_act=4, lora2_done=3, lora2_act=3, rkv_done=3, rkv_act=3,
    cum_done=1, cumx_done=1, exps=3, kk_sq=1, kk_norm=1, kk_max=1, kk_inv=1, kk_bc=1, kk_turned=1,
    prep=10, rk_ready=1, bonus_done=1, bonus_ready=1, hats_turned=2, hats_ready=2,
    scores_done=4, masked=16, eye_added=2, xt_first=2, x_first=2, x_first_ready=2,
    y_done=10, y_ready=10, z_done=10, z_ready=10, zt_done=8, zt_ready=8,
    r_done=4, r_ready=4, sa_done=4, sa_ready=4, st_done=3, decayed=2, st_ready=3, o_done=4, o_ready=1,
    gn_sum=1, gn_mean=1, gn_cent=1, gn_sq=1, gn_ss=1, gn_var=1, gn_rstd=1, gn_done=1, bv_ready=1,
    on_turned=1, on_ready=1, bv_turned=1, og_sum=1, og_ready=1, att_done=1, h2_ready=1,
    ln2_sum=1, ln2_mean=1, ln2_cent=1, ln2_sq=1, ln2_ss=1, ln2_var=1, ln2_rstd=1, ln2_rb=1, ln2_rc=1,
    ln2_rstd2=1, ln2_rr=1, ln2_done=1,
    xn_turned=1, xn_ready=1, router_done=1, top=20, gate_exp=1, gates_turned=1, gatesT_ready=1, b2_done=1,
    base_ready=1, up_done=16, act_done=16, down_done=8, weighted=8, summed=8, y_ready_out=1, y_stored=64,
)


def shape_constants():
    s, t = np.meshgrid(np.arange(P), np.arange(P), indexing="ij")
    same = s // HALF == t // HALF
    eye = (s == t)
    masks = [same & (s < t), same & (s <= t), eye | (same & (s % 2 == 0) & (t == s + 1))]
    for lvl in range(1, LEVELS + 1):
        size = 2 ** lvl
        row, col = s, t
        pair = (row // (2 * size) == col // (2 * size)) & (row // size > col // size)
        masks.append(eye | (same & pair))
    keep = np.ones((P, COLS), np.float32)
    keep[:, ::HALF] = 0.0
    small = np.zeros((P, 2 + EXPERTS + 8), np.float32)
    small[:HALF, 0] = small[HALF:, 1] = 1.0
    small[:, 2:2 + EXPERTS] = np.arange(EXPERTS, 0, -1)
    small[:, 2 + EXPERTS:] = -0.5
    return eye.astype(np.float32), np.stack(masks, 1).astype(np.float32).reshape(P, -1), keep, small


def audio_tower(nc, A, out, eye_d, masks_d, keep_d, small_d):
    QUADS = A["x"].shape[0] // QUAD
    with ExitStack() as ctx:
        def sb(name, *shape):
            return ctx.enter_context(nc.sbuf_tensor(name, [P, *shape], F32))

        S = {n: ctx.enter_context(nc.semaphore(n)) for n in PER}
        w_loaded = ctx.enter_context(nc.semaphore("w_loaded"))
        w_zeroed = ctx.enter_context(nc.semaphore("w_zeroed"))
        w_built = ctx.enter_context(nc.semaphore("w_built"))
        psum = ctx.enter_context(nc.psum_tensor("psum", [P, 8, 512], F32))
        bank = [psum[:, k, :] for k in range(8)]

        eye = sb("eye", P)
        masks = sb("masks", 3 + LEVELS, P)
        keep = sb("keep", COLS)
        filt = sb("filt", TAPS)
        wconv = sb("wconv", TAPS, D)
        bd = sb("bd", 8, P)
        W_R, W_K, W_V, W_A1, W_A2, W_W1, W_W2, W_O = range(8)
        w_g1 = sb("w_g1", P)
        w_g2 = sb("w_g2", D)
        vec = sb("vec", 16)
        (B_CONV, B_W, B_A, K_K, K_A, GN_W, GN_B, GAMMA, BETA) = range(9)
        MIX = 9
        small = sb("small", 2 + EXPERTS + 8)
        half_ones = small[:, 0:2]
        rank = small[:, 2:2 + EXPERTS]
        minus_half = small[:, 2 + EXPERTS:]
        rk_col = sb("rk_col", 2)
        w_router = sb("w_router", 2 * EXPERTS)
        router_b = sb("router_b", 2 * EXPERTS)
        w_up = sb("w_up", EXPERTS, HID)
        b_up = sb("b_up", EXPERTS)
        w_down = sb("w_down", EXPERTS, D)
        b_down = sb("b_down", P)

        xin = sb("xin", 2 * QUAD, P)
        xT = sb("xT", QUAD, 256)
        hT = sb("hT", COLS)
        h_tm = sb("h_tm", COLS)
        cent = sb("cent", COLS)
        sq = sb("sq", COLS)
        stat = sb("stat", 8, 8)
        x1_tm = sb("x1_tm", COLS)
        x1T = sb("x1T", COLS)
        delta = sb("delta", COLS)
        xm = sb("xm", 6, COLS)
        M_R, M_W, M_K, M_V, M_A, M_G = range(6)
        low = sb("low", 2, COLS)
        sig_w = sb("sig_w", COLS)
        aT = sb("aT", COLS)
        sig_g = sb("sig_g", 2, COLS)
        gT = sb("gT", COLS)
        rT = sb("rT", COLS)
        kT = sb("kT", COLS)
        v_tm = sb("v_tm", COLS)
        cum = sb("cum", COLS)
        cumx = sb("cumx", COLS)
        e_in = sb("e_in", COLS)
        e_ex = sb("e_ex", COLS)
        e_neg = sb("e_neg", COLS)
        kk2 = sb("kk2", COLS)
        inv_b = sb("inv_b", COLS)
        kkn = sb("kkn", COLS)
        ka = sb("ka", COLS)
        k2 = sb("k2", COLS)
        t1 = sb("t1", COLS)
        ar = sb("ar", 2, COLS)
        bt = sb("bt", COLS)
        kt = sb("kt", COLS)
        bh = sb("bh", COLS)
        kh = sb("kh", COLS)
        rk = sb("rk", COLS)
        bonus = sb("bonus", 8)
        bh_tm = sb("bh_tm", COLS)
        kh_tm = sb("kh_tm", COLS)
        NT = sb("NT", NCH, 2, P)
        RB = sb("RB", NCH, 2, P)
        AK = sb("AK", NCH, 2, P)
        RK = sb("RK", NCH, 2, P)
        X = sb("X", NCH, 2, P)
        XT = sb("XT", NCH, 2, P)
        Y = sb("Y", NCH, 2, P)
        r_sb = sb("r_sb", P)
        sa = sb("sa", P)
        state = sb("state", P)
        state_d = sb("state_d", P)
        o_tm = sb("o_tm", COLS)
        bv = sb("bv", COLS)
        onT = sb("onT", COLS)
        ogT = sb("ogT", COLS)
        h2 = sb("h2", COLS)
        xnT = sb("xnT", COLS)
        tops = sb("tops", 14, 8, EXPERTS)
        gate = sb("gate", NCH, 2 * EXPERTS)
        gateT = sb("gateT", COLS)
        hid = sb("hid", EXPERTS, COLS)
        prod = sb("prod", 2, 512)
        ysum = sb("ysum", COLS)
        y = sb("y", COLS)

        def fm(t):
            return t.rearrange("p (c b t) -> p c b t", c=NCH, b=2)

        def grp(t, n=8):
            return t.rearrange("p (g d) -> p g d", g=n)

        def wide(t, n=D):
            return t.unsqueeze(2).broadcast_to([P, t.shape[1], n])

        dup = [slice(0, 64), slice(64, 128)]
        n_w = 0

        block = ctx.enter_context(nc.Block())

        def nth(i, name, k=None):
            return i * PER[name] + (PER[name] if k is None else k)

        @block.sync
        def _(sp):
            loads = [
                (eye[:], eye_d), (masks[:], masks_d.rearrange("p (m t) -> p m t", t=P)), (keep[:], keep_d), (small[:], small_d),
                (filt[:], A["tok_filt"].rearrange("f d -> d f")),
                (wconv[:], A["tok_W_k"].rearrange("(f d) k -> d f k", f=TAPS)),
                (w_g2[:], A["attn_B_g"]),
                (w_down[:], A["ffn_W2"].rearrange("e h d -> h e d")),
                (b_up[:], A["ffn_b1"].rearrange("e h -> h e")),
            ]
            for a in range(2):
                loads += [
                    (w_g1[dup[a], :], A["attn_A_g"]),
                    (w_up[dup[a], :, :], A["ffn_W1"].rearrange("e d h -> d e h")),
                    (router_b[:, 8 * a:8 * a + 8], A["ffn_br"].rearrange("(o e) -> o e", o=1).broadcast_to([P, EXPERTS])),
                ]
                for k, n in enumerate(("tok_b_k", "attn_b_w", "attn_b_a", "attn_k_k", "attn_k_a",
                                       "attn_gn_w", "attn_gn_b", "ffn_gamma", "ffn_beta")):
                    loads.append((vec[dup[a], k:k + 1], A[n].rearrange("(d o) -> d o", o=1)))
                loads.append((vec[dup[a], MIX:MIX + 6], A["attn_x_mix"].rearrange("m d -> d m")))
            for dst, src in loads:
                sp.dma_start(dst, src, allow_slow_non_contiguous=True).then_inc(w_loaded, 16)
            blocks = []
            for a in range(2):
                for k, n in enumerate(("W_r", "W_k", "W_v", "A_a", "B_a", "A_w", "B_w", "W_o")):
                    blocks.append((bd[dup[a], k, dup[a]], A["attn_" + n]))
                blocks += [
                    (rk_col[dup[a], a:a + 1], A["attn_r_k"].rearrange("(d o) -> d o", o=1)),
                    (w_router[dup[a], 8 * a:8 * a + 8], A["ffn_Wr"]),
                    (b_down[8 * a:8 * a + 8, dup[a]], A["ffn_b2"]),
                ]
            sp.wait_ge(w_zeroed, 1)
            for dst, src in blocks:
                sp.dma_start(dst, src, allow_slow_non_contiguous=True).then_inc(w_loaded, 16)
            nonlocal n_w
            n_w = 16 * (len(loads) + len(blocks))
            x_q = A["x"].rearrange("s (h p) f -> p (s h) f", p=P)
            with sp.Fori(0, QUADS) as i:
                sp.wait_ge(S["x_turned"], nth(i, "x_turned", 0))
                sp.dma_start(xin[:], x_q[:, bass.ds(i * 8, 8), :]).then_inc(S["x_loaded"], 16)
            sp.wait_ge(S["y_stored"], QUADS * PER["y_stored"])

        @block.gpsimd
        def _(pool):
            for tile in (bd[:], rk_col[:], w_router[:], b_down[:], delta[:], hT[:]):
                last = nc.gpsimd.memset(tile, 0.0)
            last.then_inc(w_zeroed, 1)
            pool.wait_ge(w_loaded, n_w)

            def rsqrt(i, src, dst, ready, done):
                pool.wait_ge(S[ready], nth(i, ready))
                nc.gpsimd.tensor_tensor(stat[:, dst, :], stat[:, src, :], minus_half, ALU.pow).then_inc(S[done], 1)

            with pool.Fori(0, QUADS) as i:
                rsqrt(i, 2, 3, "ln1_var", "ln1_rstd")
                rsqrt(i, 4, 5, "kk_max", "kk_inv")
                for g in range(2):
                    cs = slice(2 * g, 2 * g + 2)
                    pool.wait_ge(S["masked"], nth(i, "masked", 8 * g + 5))
                    nc.gpsimd.tensor_tensor(
                        NT[:, cs].rearrange("p c a t -> p (c a) t"), NT[:, cs].rearrange("p c a t -> p (c a) t"),
                        eye[:].unsqueeze(1).broadcast_to([P, 4, P]), ALU.add).then_inc(S["eye_added"], 1)
                    pool.wait_ge(S["eye_added"], nth(i, "eye_added", g + 1))
                    nc.gpsimd.tensor_tensor(
                        XT[:, cs].rearrange("p c a t -> p (c a) t"), NT[:, cs].rearrange("p c a t -> p (c a) t"),
                        masks[:, 2, :].unsqueeze(1).broadcast_to([P, 4, P]), ALU.mult).then_inc(S["xt_first"], 1)
                rsqrt(i, 2, 3, "gn_var", "gn_rstd")
                rsqrt(i, 2, 3, "ln2_var", "ln2_rstd")
                rsqrt(i, 6, 7, "ln2_rc", "ln2_rstd2")

        @block.tensor
        def _(pe):
            def turn(dst, src, done):
                for c in range(NCH):
                    last = nc.tensor.transpose(dst[:, c * P:(c + 1) * P], src[:, c * P:(c + 1) * P], eye[:])
                last.then_inc(S[done], 1)

            pe.wait_ge(w_built, 1)
            pe.wait_ge(w_loaded, n_w)
            with pe.Fori(0, QUADS) as i:
                pe.wait_ge(S["x_loaded"], nth(i, "x_loaded"))
                pe.wait_ge(S["base_ready"], nth(i, "base_ready", 0))
                for s in range(2 * QUAD):
                    last = nc.tensor.transpose(bank[s // 4][:, (s % 4) * P:(s % 4 + 1) * P], xin[:, s, :], eye[:])
                last.then_inc(S["x_turned"], 1)
                pe.wait_ge(S["xT_v"], nth(i, "xT_v"))
                pe.wait_ge(S["xT_s"], nth(i, "xT_s"))
                for b in range(2):
                    for f in range(TAPS):
                        for a in range(2):
                            last = nc.tensor.matmul(bank[2][dup[a], b * 256:b * 256 + T], wconv[:, f, :],
                                                    xT[:, 2 * a + b, f:f + T], start=(f == 0), stop=(f == TAPS - 1))
                last.then_inc(S["conv_done"], 1)
                pe.wait_ge(S["h_ready"], nth(i, "h_ready"))
                turn(bank[3], hT, "h_turned")
                pe.wait_ge(S["ln1_done"], nth(i, "ln1_done"))
                turn(bank[0], x1_tm, "x1_turned")
                pe.wait_ge(S["mixed"], nth(i, "mixed", 1))
                nc.tensor.matmul(bank[4][:], bd[:, W_W1, :], xm[:, M_W, :], start=True, stop=True).then_inc(S["lora1_done"], 1)
                pe.wait_ge(S["mixed"], nth(i, "mixed", 2))
                nc.tensor.matmul(bank[5][:], bd[:, W_A1, :], xm[:, M_A, :], start=True, stop=True).then_inc(S["lora1_done"], 1)
                pe.wait_ge(S["mixed"], nth(i, "mixed", 3))
                for a in range(2):
                    nc.tensor.matmul(bank[6 + a][:], w_g1[dup[a], :], xm[dup[a], M_G, :], start=True,
                                     stop=True).then_inc(S["lora1_done"], 1)
                pe.wait_ge(S["mixed"], nth(i, "mixed", 4))
                nc.tensor.matmul(bank[2][:], bd[:, W_K, :], xm[:, M_K, :], start=True, stop=True).then_inc(S["rkv_done"], 1)
                pe.wait_ge(S["mixed"], nth(i, "mixed", 5))
                nc.tensor.matmul(bank[1][:], bd[:, W_R, :], xm[:, M_R, :], start=True, stop=True).then_inc(S["rkv_done"], 1)
                pe.wait_ge(S["mixed"], nth(i, "mixed", 6))
                for c in range(NCH):
                    last = nc.tensor.matmul(bank[3][:, c * P:(c + 1) * P], xm[:, M_V, c * P:(c + 1) * P], bd[:, W_V, :],
                                            start=True, stop=True)
                last.then_inc(S["rkv_done"], 1)
                pe.wait_ge(S["lora1_act"], nth(i, "lora1_act", 2))
                nc.tensor.matmul(bank[4][:], bd[:, W_W2, :], low[:, 0, :], start=True, stop=True).then_inc(S["lora2_done"], 1)
                nc.tensor.matmul(bank[5][:], bd[:, W_A2, :], low[:, 1, :], start=True, stop=True).then_inc(S["lora2_done"], 1)
                pe.wait_ge(S["lora1_act"], nth(i, "lora1_act", 4))
                for a in range(2):
                    last = nc.tensor.matmul(bank[6][dup[a], :], w_g2[:], sig_g[:, a, :], start=True, stop=True)
                last.then_inc(S["lora2_done"], 1)
                pe.wait_ge(S["kk_sq"], nth(i, "kk_sq"))
                for c in range(NCH):
                    last = nc.tensor.matmul(bank[7][:, 2 * c:2 * c + 2], kk2[:, c * P:(c + 1) * P], half_ones,
                                            start=True, stop=True)
                last.then_inc(S["kk_norm"], 1)
                pe.wait_ge(S["kk_bc"], nth(i, "kk_bc"))
                turn(bank[7], inv_b, "kk_turned")
                pe.wait_ge(S["lora2_act"], nth(i, "lora2_act", 2))
                pe.wait_ge(S["rkv_act"], nth(i, "rkv_act"))
                pe.wait_ge(S["prep"], nth(i, "prep", 9))
                turn(bank[0], bh, "hats_turned")
                pe.wait_ge(S["prep"], nth(i, "prep", 10))
                turn(bank[1], kh, "hats_turned")

                for g in range(2):
                    for a in range(2):
                        for cc in range(2):
                            for key, src in enumerate((bt, kt)):
                                for b in range(2):
                                    cols = slice((2 * g + cc) * P + b * HALF, (2 * g + cc) * P + b * HALF + HALF)
                                    last = nc.tensor.matmul(
                                        bank[2 + g + 2 * a][dup[b], (2 * cc + key) * P:(2 * cc + key + 1) * P].rearrange(
                                            "p (r t) -> p r t", r=2),
                                        src[dup[a], cols], ar[dup[a], :, cols], start=True, stop=True)
                        last.then_inc(S["scores_done"], 1)
                pe.wait_ge(S["rk_ready"], nth(i, "rk_ready"))
                for c in range(NCH):
                    last = nc.tensor.matmul(bank[7][:, 2 * c:2 * c + 2], rk[:, c * P:(c + 1) * P], rk_col[:],
                                            start=True, stop=True)
                last.then_inc(S["bonus_done"], 1)

                def unit(g, u):
                    return 2 * g + u // 2, u % 2

                for g in range(2):
                    pe.wait_ge(S["xt_first"], nth(i, "xt_first", g + 1))
                    pe.wait_ge(S["masked"], nth(i, "masked", 8 * g + 8))
                    for u in range(4):
                        c, a = unit(g, u)
                        last = nc.tensor.transpose(bank[2 + g][:, u * P:(u + 1) * P], XT[:, c, a, :], eye[:])
                    last.then_inc(S["x_first"], 1)
                for lvl in range(LEVELS):
                    for g in range(2):
                        if lvl == 0:
                            pe.wait_ge(S["x_first_ready"], nth(i, "x_first_ready", g + 1))
                        else:
                            pe.wait_ge(S["z_ready"], nth(i, "z_ready", 2 * (lvl - 1) + g + 1))
                        for u in range(4):
                            c, a = unit(g, u)
                            last = nc.tensor.matmul(bank[4 + g][:, u * P:(u + 1) * P], NT[:, c, a, :], X[:, c, a, :],
                                                    start=True, stop=True)
                        last.then_inc(S["y_done"], 1)
                    for g in range(2):
                        pe.wait_ge(S["y_ready"], nth(i, "y_ready", 2 * lvl + g + 1))
                        if lvl > 0:
                            pe.wait_ge(S["zt_ready"], nth(i, "zt_ready", 2 * (lvl - 1) + g + 1))
                        for u in range(4):
                            c, a = unit(g, u)
                            if lvl < LEVELS - 1:
                                w, m = XT, Y
                            else:
                                w, m = Y, XT
                            last = nc.tensor.matmul(bank[2 + g][:, u * P:(u + 1) * P], w[:, c, a, :], m[:, c, a, :],
                                                    start=True, stop=True)
                        last.then_inc(S["z_done"], 1)
                    if lvl < LEVELS - 1:
                        for g in range(2):
                            pe.wait_ge(S["z_ready"], nth(i, "z_ready", 2 * lvl + g + 1))
                            for u in range(4):
                                c, a = unit(g, u)
                                last = nc.tensor.transpose(bank[2 + g][:, u * P:(u + 1) * P], X[:, c, a, :], eye[:])
                            last.then_inc(S["zt_done"], 1)

                pe.wait_ge(S["hats_ready"], nth(i, "hats_ready"))
                pe.wait_ge(S["z_ready"], nth(i, "z_ready"))
                for c in range(NCH):
                    if c > 0:
                        pe.wait_ge(S["st_ready"], nth(i, "st_ready", c))
                    for a in range(2):
                        va = v_tm[:, c * P + a * D:c * P + a * D + D]
                        last = nc.tensor.matmul(bank[6 + a][:, 0:D], AK[:, c, a, :], va, start=True, stop=(c == 0))
                        if c > 0:
                            for b in range(2):
                                cols = slice(c * P + b * HALF, c * P + b * HALF + HALF)
                                last = nc.tensor.matmul(bank[6 + a][dup[b], 0:D], ar[dup[a], 0, cols],
                                                        state[dup[a], b * D:b * D + D], start=False, stop=True)
                    last.then_inc(S["r_done"], 1)
                    pe.wait_ge(S["r_ready"], nth(i, "r_ready", c + 1))
                    for a in range(2):
                        last = nc.tensor.matmul(bank[2][:, a * D:a * D + D], XT[:, c, a, :], r_sb[:, a * D:a * D + D],
                                                start=True, stop=True)
                    last.then_inc(S["sa_done"], 1)
                    pe.wait_ge(S["sa_ready"], nth(i, "sa_ready", c + 1))
                    for a in range(2):
                        oc = bank[4 * a][:, c * D:c * D + D]
                        va = v_tm[:, c * P + a * D:c * P + a * D + D]
                        nc.tensor.matmul(oc, RB[:, c, a, :], sa[:, a * D:a * D + D], start=True, stop=False)
                        last = nc.tensor.matmul(oc, RK[:, c, a, :], va, start=False, stop=(c == 0))
                        if c > 0:
                            for b in range(2):
                                cols = slice(c * P + b * HALF, c * P + b * HALF + HALF)
                                last = nc.tensor.matmul(bank[4 * a][dup[b], c * D:c * D + D], ar[dup[a], 1, cols],
                                                        state[dup[a], b * D:b * D + D], start=False, stop=True)
                    last.then_inc(S["o_done"], 1)
                    if c < NCH - 1:
                        for b in range(2):
                            for a in range(2):
                                kc = slice(c * P + a * D, c * P + a * D + D)
                                st = bank[1 + 4 * b][dup[a], 0:D]
                                nc.tensor.matmul(st, bh_tm[dup[b], kc], sa[dup[b], a * D:a * D + D], start=True, stop=False)
                                last = nc.tensor.matmul(st, kh_tm[dup[b], kc], v_tm[dup[b], kc], start=False, stop=True)
                        last.then_inc(S["st_done"], 1)

                pe.wait_ge(S["gn_done"], nth(i, "gn_done"))
                turn(bank[2], cent, "on_turned")
                pe.wait_ge(S["bv_ready"], nth(i, "bv_ready"))
                turn(bank[3], bv, "bv_turned")
                pe.wait_ge(S["og_ready"], nth(i, "og_ready"))
                for c in range(NCH):
                    last = nc.tensor.matmul(bank[4][:, c * P:(c + 1) * P], ogT[:, c * P:(c + 1) * P], bd[:, W_O, :],
                                            start=True, stop=True)
                last.then_inc(S["att_done"], 1)
                pe.wait_ge(S["ln2_done"], nth(i, "ln2_done"))
                turn(bank[5], cent, "xn_turned")
                pe.wait_ge(S["xn_ready"], nth(i, "xn_ready"))
                for c in range(NCH):
                    last = nc.tensor.matmul(bank[6][:, 16 * c:16 * c + 16], xnT[:, c * P:(c + 1) * P], w_router[:],
                                            start=True, stop=True)
                last.then_inc(S["router_done"], 1)

                def up(a, e):
                    n = a * EXPERTS + e
                    if n >= 2:
                        pe.wait_ge(S["act_done"], nth(i, "act_done", n - 1))
                    nc.tensor.matmul(bank[2 + n % 2][:], w_up[dup[a], e, :], xnT[dup[a], :], start=True,
                                     stop=True).then_inc(S["up_done"], 1)

                def down(a):
                    pe.wait_ge(S["act_done"], nth(i, "act_done", 8 * a + 8))
                    for c in range(NCH):
                        n = a * NCH + c
                        if n >= 2:
                            pe.wait_ge(S["weighted"], nth(i, "weighted", n - 1))
                        for e in range(EXPERTS):
                            last = nc.tensor.matmul(bank[n % 2][:, e * D:e * D + D], hid[:, e, c * P:(c + 1) * P],
                                                    w_down[:, e, :], start=True, stop=True)
                        last.then_inc(S["down_done"], 1)

                for e in range(EXPERTS):
                    up(0, e)
                down(0)
                for e in range(EXPERTS):
                    up(1, e)
                down(1)
                pe.wait_ge(S["top"], nth(i, "top"))
                for c in range(NCH):
                    last = nc.tensor.transpose(bank[7][0:16, c * P:(c + 1) * P], gate[:, c, :], eye[:])
                last.then_inc(S["gates_turned"], 1)
                pe.wait_ge(S["gatesT_ready"], nth(i, "gatesT_ready"))
                for c in range(NCH):
                    last = nc.tensor.matmul(bank[5][:, c * P:(c + 1) * P], gateT[0:16, c * P:(c + 1) * P], b_down[0:16, :],
                                            start=True, stop=True)
                last.then_inc(S["b2_done"], 1)

        @block.scalar
        def _(act):
            def v(k):
                return vec[:, k:k + 1]

            act.wait_ge(w_zeroed, 1)
            act.wait_ge(w_loaded, n_w)
            with act.Fori(0, QUADS) as i:
                act.wait_ge(S["x_turned"], nth(i, "x_turned"))
                nc.scalar.copy(xT[:, 2:4, :].rearrange("p s t -> p (s t)"), bank[1][:]).then_inc(S["xT_s"], 1)
                act.wait_ge(S["conv_done"], nth(i, "conv_done"))
                for b in range(2):
                    last = nc.scalar.activation(
                        fm(hT[:])[:, :, b, 0:CHUNK], bank[2][:, b * 256:b * 256 + T].rearrange("p (c t) -> p c t", c=NCH),
                        ACT.Relu, bias=v(B_CONV))
                last.then_inc(S["h_ready"], 1)
                act.wait_ge(S["h_turned"], nth(i, "h_turned"))
                nc.scalar.copy(h_tm[:], bank[3][:]).then_inc(S["htm_ready"], 1)
                act.wait_ge(S["ln1_cent"], nth(i, "ln1_cent"))
                nc.scalar.activation(sq[:], cent[:], ACT.Square).then_inc(S["ln1_sq"], 1)
                act.wait_ge(S["x1_turned"], nth(i, "x1_turned"))
                nc.scalar.copy(x1T[:], bank[0][:]).then_inc(S["x1T_ready"], 1)
                act.wait_ge(S["lora1_done"], nth(i, "lora1_done", 1))
                nc.scalar.activation(low[:, 0, :], bank[4][:], ACT.Tanh).then_inc(S["lora1_act"], 1)
                act.wait_ge(S["lora1_done"], nth(i, "lora1_done", 2))
                nc.scalar.copy(low[:, 1, :], bank[5][:]).then_inc(S["lora1_act"], 1)
                for a in range(2):
                    act.wait_ge(S["lora1_done"], nth(i, "lora1_done", 3 + a))
                    nc.scalar.activation(sig_g[:, a, :], bank[6 + a][:], ACT.Sigmoid).then_inc(S["lora1_act"], 1)
                act.wait_ge(S["rkv_done"], nth(i, "rkv_done", 1))
                nc.scalar.copy(kT[:], bank[2][:]).then_inc(S["rkv_act"], 1)
                nc.scalar.activation(kk2[:], bank[2][:], ACT.Square, scale=v(K_K)).then_inc(S["kk_sq"], 1)
                act.wait_ge(S["lora2_done"], nth(i, "lora2_done", 1))
                nc.scalar.activation(sig_w[:], bank[4][:], ACT.Sigmoid, bias=v(B_W)).then_inc(S["lora2_act"], 1)
                act.wait_ge(S["lora2_done"], nth(i, "lora2_done", 2))
                nc.scalar.activation(aT[:], bank[5][:], ACT.Sigmoid, bias=v(B_A)).then_inc(S["lora2_act"], 1)
                act.wait_ge(S["rkv_done"], nth(i, "rkv_done", 2))
                nc.scalar.copy(rT[:], bank[1][:]).then_inc(S["rkv_act"], 1)
                act.wait_ge(S["rkv_done"], nth(i, "rkv_done", 3))
                nc.scalar.copy(v_tm[:], bank[3][:]).then_inc(S["rkv_act"], 1)
                act.wait_ge(S["lora2_done"], nth(i, "lora2_done", 3))
                nc.scalar.copy(gT[:], bank[6][:]).then_inc(S["lora2_act"], 1)
                act.wait_ge(S["cum_done"], nth(i, "cum_done"))
                nc.scalar.activation(e_neg[:], cum[:], ACT.Exp, scale=-DECAY_SCALE).then_inc(S["exps"], 1)
                nc.scalar.activation(e_in[:], cum[:], ACT.Exp, scale=DECAY_SCALE).then_inc(S["exps"], 1)
                act.wait_ge(S["cumx_done"], nth(i, "cumx_done"))
                nc.scalar.activation(e_ex[:], cumx[:], ACT.Exp, scale=DECAY_SCALE).then_inc(S["exps"], 1)
                act.wait_ge(S["hats_turned"], nth(i, "hats_turned", 1))
                nc.scalar.copy(bh_tm[:], bank[0][:]).then_inc(S["hats_ready"], 1)
                act.wait_ge(S["hats_turned"], nth(i, "hats_turned", 2))
                nc.scalar.copy(kh_tm[:], bank[1][:]).then_inc(S["hats_ready"], 1)

                def group(t, g):
                    return t[:, 2 * g:2 * g + 2].rearrange("p c a t -> p (c a t)")

                for g in range(2):
                    act.wait_ge(S["x_first"], nth(i, "x_first", g + 1))
                    nc.scalar.copy(group(X, g), bank[2 + g][:]).then_inc(S["x_first_ready"], 1)
                for lvl in range(LEVELS):
                    for g in range(2):
                        act.wait_ge(S["z_done"], nth(i, "z_done", 2 * lvl + g + 1))
                        dst = X if lvl < LEVELS - 1 else XT
                        nc.scalar.copy(group(dst, g), bank[2 + g][:]).then_inc(S["z_ready"], 1)
                    if lvl < LEVELS - 1:
                        for g in range(2):
                            act.wait_ge(S["zt_done"], nth(i, "zt_done", 2 * lvl + g + 1))
                            nc.scalar.copy(group(XT, g), bank[2 + g][:]).then_inc(S["zt_ready"], 1)
                for c in range(NCH):
                    act.wait_ge(S["r_done"], nth(i, "r_done", c + 1))
                    nc.scalar.copy(grp(r_sb[:], 2), psum[:, 6:8, 0:D]).then_inc(S["r_ready"], 1)
                act.wait_ge(S["o_done"], nth(i, "o_done"))
                nc.scalar.copy(o_tm[:].rearrange("p (c a d) -> p a c d", c=NCH, a=2),
                               psum[:, 0:5:4, 0:NCH * D].rearrange("p a (c d) -> p a c d", c=NCH)).then_inc(S["o_ready"], 1)
                act.wait_ge(S["gn_cent"], nth(i, "gn_cent"))
                nc.scalar.activation(sq[:], cent[:], ACT.Square).then_inc(S["gn_sq"], 1)
                act.wait_ge(S["on_turned"], nth(i, "on_turned"))
                nc.scalar.activation(onT[:], bank[2][:], ACT.Identity, scale=v(GN_W), bias=v(GN_B)).then_inc(S["on_ready"], 1)
                act.wait_ge(S["ln2_cent"], nth(i, "ln2_cent"))
                nc.scalar.activation(sq[:], cent[:], ACT.Square).then_inc(S["ln2_sq"], 1)
                act.wait_ge(S["xn_turned"], nth(i, "xn_turned"))
                nc.scalar.activation(xnT[:], bank[5][:], ACT.Identity, scale=v(GAMMA), bias=v(BETA)).then_inc(S["xn_ready"], 1)
                for a in range(2):
                    if a == 1:
                        act.wait_ge(S["down_done"], nth(i, "down_done", NCH))
                    for e in range(EXPERTS):
                        n = a * EXPERTS + e
                        act.wait_ge(S["up_done"], nth(i, "up_done", n + 1))
                        nc.scalar.activation(hid[:, e, :], bank[2 + n % 2][:], ACT.Gelu,
                                             bias=b_up[:, e:e + 1]).then_inc(S["act_done"], 1)
                    if a == 0:
                        act.wait_ge(S["top"], nth(i, "top", 15))
                        nc.scalar.activation(tops[:, 6, :, 0], tops[:, 5, :, 0], ACT.Tanh,
                                             scale=0.5).then_inc(S["gate_exp"], 1)
                act.wait_ge(S["gates_turned"], nth(i, "gates_turned"))
                nc.scalar.copy(gateT[0:16, :], bank[7][0:16, :]).then_inc(S["gatesT_ready"], 1)
                act.wait_ge(S["y_ready_out"], nth(i, "y_ready_out"))
                yv = y[:].rearrange("p (c a d) -> p c a d", c=NCH, a=2)
                for b in range(2):
                    for a in range(2):
                        act.dma_start(
                            out[bass.ds(i * QUAD + 2 * a + b, 1), :, :].rearrange("s (c t) d -> t (s c) d", c=NCH),
                            yv[b * HALF:b * HALF + CHUNK, :, a, :]).then_inc(S["y_stored"], 16)

        @block.vector
        def _(dve):
            tt, ts, stt = nc.vector.tensor_tensor, nc.vector.tensor_scalar, nc.vector.scalar_tensor_tensor

            def v(k):
                return vec[:, k:k + 1]

            def moments(i, src, name, ready, eps):
                dve.wait_ge(S[ready], nth(i, ready))
                nc.vector.reduce_sum(stat[:, 0, :], grp(src[:]), AX_X).then_inc(S[name + "_sum"], 1)
                dve.wait_ge(S[name + "_sum"], nth(i, name + "_sum"))
                ts(stat[:, 1, :], stat[:, 0, :], -1.0 / D, None, ALU.mult).then_inc(S[name + "_mean"], 1)
                dve.wait_ge(S[name + "_mean"], nth(i, name + "_mean"))
                tt(grp(cent[:]), grp(src[:]), wide(stat[:, 1, :]), ALU.add).then_inc(S[name + "_cent"], 1)
                dve.wait_ge(S[name + "_sq"], nth(i, name + "_sq"))
                nc.vector.reduce_sum(stat[:, 0, :], grp(sq[:]), AX_X).then_inc(S[name + "_ss"], 1)
                dve.wait_ge(S[name + "_ss"], nth(i, name + "_ss"))
                ts(stat[:, 2, :], stat[:, 0, :], 1.0 / D, eps, ALU.mult, ALU.add).then_inc(S[name + "_var"], 1)

            dve.wait_ge(w_zeroed, 1)
            dve.wait_ge(w_loaded, n_w)
            tt(wconv[:], wconv[:], filt[:].unsqueeze(2).broadcast_to([P, TAPS, D]), ALU.mult).then_inc(w_built, 1)
            dve.wait_ge(w_built, 1)
            with dve.Fori(0, QUADS) as i:
                dve.wait_ge(S["x_turned"], nth(i, "x_turned"))
                nc.vector.tensor_copy(xT[:, 0:2, :].rearrange("p s t -> p (s t)"), bank[0][:]).then_inc(S["xT_v"], 1)
                moments(i, h_tm, "ln1", "htm_ready", LN_EPS)
                dve.wait_ge(S["ln1_rstd"], nth(i, "ln1_rstd"))
                tt(grp(x1_tm[:]), grp(cent[:]), wide(stat[:, 3, :]), ALU.mult).then_inc(S["ln1_done"], 1)
                dve.wait_ge(S["x1T_ready"], nth(i, "x1T_ready"))
                xv, dv = fm(x1T[:]), fm(delta[:])
                tt(dv[:, :, :, 1:CHUNK], xv[:, :, :, 0:CHUNK - 1], xv[:, :, :, 1:CHUNK], ALU.subtract).then_inc(S["delta_ready"], 1)
                tt(dv[:, 1:NCH, :, 0], xv[:, 0:NCH - 1, :, CHUNK - 1], xv[:, 1:NCH, :, 0], ALU.subtract).then_inc(S["delta_ready"], 1)
                ts(dv[:, 0, :, 0], xv[:, 0, :, 0], -1.0, None, ALU.mult).then_inc(S["delta_ready"], 1)
                dve.wait_ge(S["delta_ready"], nth(i, "delta_ready"))
                for m in (M_W, M_A, M_G, M_K, M_R, M_V):
                    stt(xm[:, m, :], delta[:], v(MIX + m), x1T[:], ALU.mult, ALU.add).then_inc(S["mixed"], 1)
                dve.wait_ge(S["kk_norm"], nth(i, "kk_norm"))
                ts(stat[:, 4, :], bank[7][:, 0:8], 1e-24, None, ALU.max).then_inc(S["kk_max"], 1)
                dve.wait_ge(S["lora2_act"], nth(i, "lora2_act", 1))
                nc.vector.tensor_tensor_scan(cum[:], keep[:], sig_w[:], 0.0, ALU.mult, ALU.add).then_inc(S["cum_done"], 1)
                dve.wait_ge(S["cum_done"], nth(i, "cum_done"))
                tt(cumx[:], cum[:], sig_w[:], ALU.subtract).then_inc(S["cumx_done"], 1)
                dve.wait_ge(S["kk_inv"], nth(i, "kk_inv"))
                nc.vector.tensor_copy(grp(inv_b[:]), wide(stat[:, 5, :])).then_inc(S["kk_bc"], 1)
                dve.wait_ge(S["lora2_act"], nth(i, "lora2_act", 2))
                ts(t1[:], aT[:], 1.0, v(K_A), ALU.subtract, ALU.mult).then_inc(S["prep"], 1)
                dve.wait_ge(S["prep"], nth(i, "prep", 1))
                dve.wait_ge(S["rkv_act"], nth(i, "rkv_act"))
                stt(k2[:], t1[:], 1.0, kT[:], ALU.add, ALU.mult).then_inc(S["prep"], 1)
                dve.wait_ge(S["kk_turned"], nth(i, "kk_turned"))
                stt(kkn[:], kT[:], v(K_K), bank[7][:], ALU.mult, ALU.mult).then_inc(S["prep"], 1)
                dve.wait_ge(S["prep"], nth(i, "prep", 3))
                tt(ka[:], kkn[:], aT[:], ALU.mult).then_inc(S["prep"], 1)
                dve.wait_ge(S["exps"], nth(i, "exps"))
                tt(kt[:], k2[:], e_neg[:], ALU.mult).then_inc(S["prep"], 1)
                dve.wait_ge(S["prep"], nth(i, "prep", 5))
                tt(bt[:], ka[:], e_neg[:], ALU.mult).then_inc(S["prep"], 1)
                stt(ar[:, 0, :], kkn[:], -1.0, e_ex[:], ALU.mult, ALU.mult).then_inc(S["prep"], 1)
                tt(ar[:, 1, :], rT[:], e_in[:], ALU.mult).then_inc(S["prep"], 1)
                dve.wait_ge(S["prep"], nth(i, "prep", 6))
                last_decay = fm(e_in[:])[:, :, :, CHUNK - 1].rearrange("p c b -> p (c b)")
                tt(grp(bh[:]), grp(bt[:]), wide(last_decay), ALU.mult).then_inc(S["prep"], 1)
                tt(grp(kh[:]), grp(kt[:]), wide(last_decay), ALU.mult).then_inc(S["prep"], 1)
                tt(rk[:], rT[:], k2[:], ALU.mult).then_inc(S["rk_ready"], 1)

                for g in range(2):
                    for a in range(2):
                        dve.wait_ge(S["scores_done"], nth(i, "scores_done", 2 * g + a + 1))
                        both = bank[2 + g + 2 * a][:].rearrange("p (c k r t) -> p c k r t", c=2, k=2, r=2)
                        for key, r, dst in ((0, 0, NT), (0, 1, RB), (1, 0, AK), (1, 1, RK)):
                            tt(dst[:, 2 * g:2 * g + 2, a, :].rearrange("p c (b t) -> p c b t", b=2),
                               both[:, :, key, r, :].unsqueeze(2).broadcast_to([P, 2, 2, HALF]),
                               masks[:, r, :].rearrange("p (b t) -> p b t", b=2).unsqueeze(1).broadcast_to([P, 2, 2, HALF]),
                               ALU.mult).then_inc(S["masked"], 1)
                dve.wait_ge(S["bonus_done"], nth(i, "bonus_done"))
                nc.vector.tensor_copy(bonus[:], bank[7][:, 0:8]).then_inc(S["bonus_ready"], 1)
                for lvl in range(LEVELS):
                    for g in range(2):
                        dve.wait_ge(S["y_done"], nth(i, "y_done", 2 * lvl + g + 1))
                        tt(Y[:, 2 * g:2 * g + 2].rearrange("p c a t -> p (c a) t"), grp(bank[4 + g][:], 4),
                           masks[:, 3 + lvl, :].unsqueeze(1).broadcast_to([P, 4, P]), ALU.mult).then_inc(S["y_ready"], 1)

                for c in range(NCH):
                    if c in (1, 2):
                        dve.wait_ge(S["st_ready"], nth(i, "st_ready", c))
                        tt(grp(state_d[:], 2), grp(state[:], 2), wide(fm(e_in[:])[:, c, :, CHUNK - 1]),
                           ALU.mult).then_inc(S["decayed"], 1)
                    dve.wait_ge(S["sa_done"], nth(i, "sa_done", c + 1))
                    nc.vector.tensor_copy(sa[:], bank[2][:, 0:P]).then_inc(S["sa_ready"], 1)
                    if c < NCH - 1:
                        dve.wait_ge(S["st_done"], nth(i, "st_done", c + 1))
                        if c > 0:
                            dve.wait_ge(S["decayed"], nth(i, "decayed", c))
                        new = psum[:, 1:6:4, 0:D]
                        if c == 0:
                            nc.vector.tensor_copy(grp(state[:], 2), new).then_inc(S["st_ready"], 1)
                        else:
                            tt(grp(state[:], 2), grp(state_d[:], 2), new, ALU.add).then_inc(S["st_ready"], 1)

                moments(i, o_tm, "gn", "o_ready", GN_EPS)
                dve.wait_ge(S["bonus_ready"], nth(i, "bonus_ready"))
                tt(grp(bv[:]), grp(v_tm[:]), wide(bonus[:]), ALU.mult).then_inc(S["bv_ready"], 1)
                dve.wait_ge(S["gn_rstd"], nth(i, "gn_rstd"))
                tt(grp(cent[:]), grp(cent[:]), wide(stat[:, 3, :]), ALU.mult).then_inc(S["gn_done"], 1)
                dve.wait_ge(S["bv_turned"], nth(i, "bv_turned"))
                dve.wait_ge(S["on_ready"], nth(i, "on_ready"))
                tt(onT[:], onT[:], bank[3][:], ALU.add).then_inc(S["og_sum"], 1)
                dve.wait_ge(S["og_sum"], nth(i, "og_sum"))
                tt(ogT[:], onT[:], gT[:], ALU.mult).then_inc(S["og_ready"], 1)
                dve.wait_ge(S["att_done"], nth(i, "att_done"))
                tt(h2[:], h_tm[:], bank[4][:], ALU.add).then_inc(S["h2_ready"], 1)
                moments(i, h2, "ln2", "h2_ready", LN_EPS)
                dve.wait_ge(S["ln2_rstd"], nth(i, "ln2_rstd"))
                dve.wait_ge(S["ln2_var"], nth(i, "ln2_var"))
                ts(stat[:, 5, :], stat[:, 2, :], LN_EPS, None, ALU.subtract).then_inc(S["ln2_rb"], 1)
                tt(stat[:, 4, :], stat[:, 3, :], stat[:, 3, :], ALU.mult).then_inc(S["ln2_rr"], 1)
                dve.wait_ge(S["ln2_rr"], nth(i, "ln2_rr"))
                tt(stat[:, 5, :], stat[:, 4, :], stat[:, 5, :], ALU.mult).then_inc(S["top"], 1)
                dve.wait_ge(S["top"], nth(i, "top", 1))
                ts(stat[:, 6, :], stat[:, 5, :], LN_EPS, None, ALU.add).then_inc(S["ln2_rc"], 1)
                dve.wait_ge(S["ln2_rstd2"], nth(i, "ln2_rstd2"))
                tt(stat[:, 4, :], stat[:, 3, :], stat[:, 7, :], ALU.mult).then_inc(S["top"], 1)
                dve.wait_ge(S["top"], nth(i, "top", 2))
                tt(grp(cent[:]), grp(cent[:]), wide(stat[:, 4, :]), ALU.mult).then_inc(S["ln2_done"], 1)

                step = [2]

                def top(ins):
                    step[0] += 1
                    ins.then_inc(S["top"], 1)
                    dve.wait_ge(S["top"], nth(i, "top", step[0]))

                L, EQ, EQ2, T1, T2, DIFF = (tops[:, k] for k in range(6))
                TH = tops[:, 6]
                F1, F2, MX, L2 = (tops[:, k] for k in (7, 8, 9, 10))
                W1, W2 = tops[:, 11], tops[:, 12]
                G = gate[:].rearrange("p c (a e) -> p (c a) e", a=2)

                def one(t):
                    return t[:, :, 0:1].broadcast_to([P, 8, EXPERTS])

                ranks = rank.unsqueeze(1).broadcast_to([P, 8, EXPERTS])
                dve.wait_ge(S["router_done"], nth(i, "router_done"))
                top(tt(L.rearrange("p (c a) e -> p c (a e)", a=2), bank[6][:, 0:64].rearrange("p (c e) -> p c e", c=NCH),
                       router_b[:].unsqueeze(1).broadcast_to([P, NCH, 16]), ALU.add))
                top(nc.vector.tensor_reduce(T1[:, :, 0], L, AX_X, ALU.max))
                top(tt(EQ, L, one(T1), ALU.is_equal))
                top(tt(EQ, EQ, ranks, ALU.mult))
                top(nc.vector.tensor_reduce(MX[:, :, 0], EQ, AX_X, ALU.max))
                top(tt(F1, EQ, one(MX), ALU.is_equal))
                top(stt(L2, F1, -3e38, L, ALU.mult, ALU.add))
                top(nc.vector.tensor_reduce(T2[:, :, 0], L2, AX_X, ALU.max))
                top(tt(EQ2, L2, one(T2), ALU.is_equal))
                top(tt(EQ2, EQ2, ranks, ALU.mult))
                top(nc.vector.tensor_reduce(MX[:, :, 0], EQ2, AX_X, ALU.max))
                top(tt(F2, EQ2, one(MX), ALU.is_equal))
                top(tt(DIFF[:, :, 0], T2[:, :, 0], T1[:, :, 0], ALU.subtract))
                dve.wait_ge(S["gate_exp"], nth(i, "gate_exp"))
                top(ts(W1[:, :, 0], TH[:, :, 0], -0.5, 0.5, ALU.mult, ALU.add))
                top(ts(W2[:, :, 0], TH[:, :, 0], 0.5, 0.5, ALU.mult, ALU.add))
                top(tt(G, F1, one(W1), ALU.mult))
                top(tt(F2, F2, one(W2), ALU.mult))
                top(tt(G, G, F2, ALU.add))
                for a in range(2):
                    for c in range(NCH):
                        n = a * NCH + c
                        dve.wait_ge(S["down_done"], nth(i, "down_done", n + 1))
                        tt(prod[:, n % 2, :].rearrange("p (e d) -> p e d", e=EXPERTS),
                           bank[n % 2][:].rearrange("p (e d) -> p e d", e=EXPERTS),
                           gate[:, c, 8 * a:8 * a + 8].unsqueeze(2).broadcast_to([P, EXPERTS, D]),
                           ALU.mult).then_inc(S["weighted"], 1)
                        dve.wait_ge(S["weighted"], nth(i, "weighted", n + 1))
                        nc.vector.reduce_sum(ysum[:, c * P + a * D:c * P + a * D + D],
                                             prod[:, n % 2, :].rearrange("p (e d) -> p d e", e=EXPERTS),
                                             AX_X).then_inc(S["summed"], 1)
                dve.wait_ge(S["b2_done"], nth(i, "b2_done"))
                dve.wait_ge(S["summed"], nth(i, "summed"))
                tt(ysum[:], ysum[:], bank[5][:], ALU.add).then_inc(S["base_ready"], 1)
                dve.wait_ge(S["base_ready"], nth(i, "base_ready"))
                dve.wait_ge(S["y_stored"], nth(i, "y_stored", 0))
                tt(y[:], ysum[:], h2[:], ALU.add).then_inc(S["y_ready_out"], 1)


_INS = ["x", "L0_tok_filt", "L0_tok_W_k", "L0_tok_b_k", "L0_attn_x_mix", "L0_attn_W_r", "L0_attn_W_k", "L0_attn_W_v",
        "L0_attn_W_o", "L0_attn_A_w", "L0_attn_B_w", "L0_attn_b_w", "L0_attn_A_a", "L0_attn_B_a", "L0_attn_b_a",
        "L0_attn_A_g", "L0_attn_B_g", "L0_attn_k_k", "L0_attn_k_a", "L0_attn_r_k", "L0_attn_gn_w", "L0_attn_gn_b",
        "L0_ffn_gamma", "L0_ffn_beta", "L0_ffn_Wr", "L0_ffn_br", "L0_ffn_W1", "L0_ffn_b1", "L0_ffn_W2", "L0_ffn_b2"]


def kernel(**inputs):
    import concourse.bacc as _bacc
    from concourse.bass_utils import run_bass_kernel_spmd as _run

    nc = _bacc.Bacc("TRN2", target_bir_lowering=False, num_devices=1)
    arrays, args = {}, {}
    for name in _INS:
        a = np.ascontiguousarray(inputs[name])
        arrays[f"in_{name}"] = a
        args[name.replace("L0_", "")] = nc.dram_tensor(f"in_{name}", a.shape, mybir.dt.from_np(a.dtype), kind="ExternalInput").ap()
    consts = []
    for k, a in enumerate(shape_constants()):
        arrays[f"const_{k}"] = a
        consts.append(nc.dram_tensor(f"const_{k}", a.shape, F32, kind="ExternalInput").ap())
    out = nc.dram_tensor("out", (inputs["x"].shape[0], T, D), F32, kind="ExternalOutput").ap()
    audio_tower(nc, args, out, *consts)
    r = _run(nc, [arrays], core_ids=[0])
    return r.results[0]["out"]
```

```python
from contextlib import ExitStack

import numpy as np

import concourse.bass as bass
from concourse import mybir

F32 = mybir.dt.float32
BF16 = mybir.dt.bfloat16
ALU = mybir.AluOpType
ACT = mybir.ActivationFunctionType
AX_X = mybir.AxisListType.X

P = 128
D = 64
HALF = 64
TAPS = 8
CHUNK = 62
NCH = 4
T = CHUNK * NCH
QUAD = 4
COLS = NCH * P
EXPERTS = 8
HID = 128
LEVELS = 5
DECAY_SCALE = -0.6065306597126334
LN_EPS = 1e-5
GN_EPS = D * 1e-5


PER = dict(
    x_loaded=16, x_turned=2, xT_ready_v=1, xT_ready_s=1, conv_done=2, h_ready=2, h_turned=1, htm_ready=1,
    ln1_sum=1, ln1_mean=1, ln1_cent=1, ln1_sq=1, ln1_ss=1, ln1_var=1, ln1_rstd=1, ln1_done=1,
    x1_turned=1, x1T_ready=1, delta_ready=3, mixed=6,
    w_proj=2, w_act=2, a_proj=2, a_act=2, g_proj=3, g_act=3, k_proj=1, k_act=1, kk_sq=1, r_proj=1, r_act=1,
    v_proj=1, v_act=1, cum_done=1, cumx_done=1, exps=3, kk_norm=1, kk_max=1, kk_inv=1, kk_bc=1, kk_turned=1,
    prep=10, rk_ready=1, bonus_done=1, bonus_ready=1, hats_turned=2, hats_ready=2,
    scores_done=4, masked=16, eye_added=2, xt_first=2, x_first=2, x_first_ready=2,
    y_done=10, y_ready=10, z_done=10, z_ready=10, zt_done=8, zt_ready=8,
    r_done=4, r_ready=4, sa_done=4, sa_ready=4, st_done=3, decayed=2, st_ready=6, o_done=1, o_ready=1,
    gn_sum=1, gn_mean=1, gn_cent=1, gn_sq=1, gn_ss=1, gn_var=1, gn_rstd=1, gn_done=1, bv_ready=1,
    on_turned=1, on_ready=1, bv_turned=1, og_sum=1, og_ready=1, att_done=1, h2_ready=1,
    ln2_sum=1, ln2_mean=1, ln2_cent=1, ln2_sq=1, ln2_ss=1, ln2_var=1, ln2_rstd=1, ln2_var0=1, ln2_rr=1,
    ln2_ratio=1, ln2_var2=1, ln2_rstd2=1, ln2_scale=1, ln2_done=1,
    xn_turned=1, xn_ready=1, router_done=1, top=23, gate_tanh=1, gates_turned=1, gatesT_ready=1,
    up_done=16, act_done=16, spread_done=16, weighted=16, down_done=8, ffn_ready=1, ffn_turned=1,
    out_ready=1, y_stored=64,
)
SMALL = dict(half_ones=(0, 2), rank=(2, 8), minus_half=(10, 8), gate_row=(18, 16))


def shape_constants():
    s, t = np.meshgrid(np.arange(P), np.arange(P), indexing="ij")
    same = s // HALF == t // HALF
    eye = (s == t)
    masks = [same & (s < t), same & (s <= t), eye | (same & (s % 2 == 0) & (t == s + 1))]
    for lvl in range(1, LEVELS + 1):
        size = 2 ** lvl
        masks.append(eye | (same & (s // (2 * size) == t // (2 * size)) & (s // size > t // size)))
    keep = np.ones((P, COLS), np.float32)
    keep[:, ::HALF] = 0.0
    small = np.zeros((P, 34), np.float32)
    small[:HALF, 0] = small[HALF:, 1] = 1.0
    small[:, 2:10] = np.arange(EXPERTS, 0, -1)
    small[:, 10:18] = -0.5
    for n in range(2 * EXPERTS):
        a, e = n % 2, n // 2
        for part in range(3):
            small[32 * part + 8 * a + e, 18 + n] = 1.0
    return eye.astype(np.float32), np.stack(masks, 1).astype(np.float32).reshape(P, -1), keep, small


def audio_tower(nc, A, out, eye_d, masks_d, keep_d, small_d):
    QUADS = A["x"].shape[0] // QUAD
    SLOTS = 2 * EXPERTS + 2
    with ExitStack() as ctx:
        def sb(name, *shape, dt=F32):
            return ctx.enter_context(nc.sbuf_tensor(name, [P, *shape], dt))

        S = {n: ctx.enter_context(nc.semaphore(n)) for n in PER}
        c_loaded, w_loaded, w_zeroed, w_built = (
            ctx.enter_context(nc.semaphore(n)) for n in ("c_loaded", "w_loaded", "w_zeroed", "w_built"))
        psum = ctx.enter_context(nc.psum_tensor("psum", [P, 8, 512], F32))
        bank = [psum[:, k, :] for k in range(8)]

        eye = sb("eye", P)
        eye_h = sb("eye_h", P, dt=BF16)
        masks = sb("masks", 3 + LEVELS, P)
        keep = sb("keep", COLS)
        small = sb("small", 34)
        half_ones, rank, minus_half, gate_row = (small[:, o:o + n] for o, n in SMALL.values())
        filt = sb("filt", TAPS)
        wconv = sb("wconv", TAPS, D)
        bd = sb("bd", 8, P)
        W_R, W_K, W_V, W_A1, W_A2, W_W1, W_W2, W_O = range(8)
        w_g1 = sb("w_g1", P)
        w_g2 = sb("w_g2", D)
        vec = sb("vec", 16)
        (B_CONV, B_W, B_A, K_K, K_A, GN_W, GN_B, GAMMA, BETA) = range(9)
        MIX = 9
        rk_col = sb("rk_col", 2)
        w_router = sb("w_router", 2 * EXPERTS)
        router_b = sb("router_b", 2 * EXPERTS)
        w_up = sb("w_up", EXPERTS, HID)
        b_up = sb("b_up", EXPERTS)
        w_down = sb("w_down", EXPERTS, D)
        b_down = sb("b_down", P)
        b_rest = sb("b_rest", P)
        b_parts = sb("b_parts", 3, P, dt=BF16)
        spread = sb("spread", 2 * EXPERTS, P, dt=BF16)

        xin = sb("xin", 2 * QUAD, P)
        xT = sb("xT", QUAD, 256)
        hT = sb("hT", COLS)
        h_tm = sb("h_tm", COLS)
        cent1, cent2, cent_g = sb("cent1", COLS), sb("cent2", COLS), sb("cent_g", COLS)
        sq1, sq2, sq_g = sb("sq1", COLS), sb("sq2", COLS), sb("sq_g", COLS)
        st1, st2, st_g, st_k = sb("st1", 4, 8), sb("st2", 9, 8), sb("st_g", 4, 8), sb("st_k", 2, 8)
        x1_tm = sb("x1_tm", COLS)
        x1T = sb("x1T", COLS)
        delta = sb("delta", COLS)
        xm = sb("xm", 6, COLS)
        M_R, M_W, M_K, M_V, M_A, M_G = range(6)
        low_w, low_a = sb("low_w", COLS), sb("low_a", COLS)
        sig_w, aT = sb("sig_w", COLS), sb("aT", COLS)
        sig_g = sb("sig_g", 2, COLS)
        gT, rT, kT, v_tm = sb("gT", COLS), sb("rT", COLS), sb("kT", COLS), sb("v_tm", COLS)
        cum, cumx = sb("cum", COLS), sb("cumx", COLS)
        e_in, e_ex, e_neg = sb("e_in", COLS), sb("e_ex", COLS), sb("e_neg", COLS)
        kk2, inv_b, kkn, ka = sb("kk2", COLS), sb("inv_b", COLS), sb("kkn", COLS), sb("ka", COLS)
        k2, t1 = sb("k2", COLS), sb("t1", COLS)
        ar = sb("ar", 2, COLS)
        bt, kt, bh, kh, rk = sb("bt", COLS), sb("kt", COLS), sb("bh", COLS), sb("kh", COLS), sb("rk", COLS)
        bonus = sb("bonus", 8)
        bh_tm, kh_tm = sb("bh_tm", COLS), sb("kh_tm", COLS)
        NT, RB, AK, RK = (sb(n, NCH, 2, P) for n in ("NT", "RB", "AK", "RK"))
        X, XT, Y = (sb(n, NCH, 2, P) for n in ("X", "XT", "Y"))
        r_sb, sa = sb("r_sb", P), sb("sa", P)
        state, state_d = sb("state", 2, P), sb("state_d", 2, P)
        o_tm = sb("o_tm", COLS)
        bv, onT, ogT, h2, xnT = sb("bv", COLS), sb("onT", COLS), sb("ogT", COLS), sb("h2", COLS), sb("xnT", COLS)
        tops = sb("tops", 13, 8, EXPERTS)
        gate, gate_rest = sb("gate", NCH, 2 * EXPERTS), sb("gate_rest", NCH, 2 * EXPERTS)
        gate_parts = sb("gate_parts", NCH, P, dt=BF16)
        gateT = sb("gateT", COLS, dt=BF16)
        hid, hidw = sb("hid", 2, COLS), sb("hidw", 2, COLS)
        ffnT = sb("ffnT", COLS)
        y = sb("y", COLS)

        def fm(t):
            return t.rearrange("p (c b t) -> p c b t", c=NCH, b=2)

        def grp(t, n=8):
            return t.rearrange("p (g d) -> p g d", g=n)

        def wide(t, n=D):
            return t.unsqueeze(2).broadcast_to([P, t.shape[1], n])

        def group(t, g):
            return t[:, 2 * g:2 * g + 2].rearrange("p c a t -> p (c a) t")

        def four(t):
            return t.unsqueeze(1).broadcast_to([P, 4, P])

        dup = [slice(0, 64), slice(64, 128)]
        n_c = n_w = 0

        block = ctx.enter_context(nc.Block())

        def nth(q, name, k=None):
            reg, off = q if isinstance(q, tuple) else (None, q)
            const = off * PER[name] + (PER[name] if k is None else k)
            return const if reg is None else reg * PER[name] + const

        def later(q):
            return isinstance(q, tuple) or q > 0

        def before(q):
            return (q[0], q[1] - 1) if isinstance(q, tuple) else q - 1

        def pipeline(eng, iteration):
            iteration(0, None)
            iteration(1, 0)
            if QUADS > 2:
                with eng.Fori(2, QUADS) as i:
                    iteration((i, 0), (i, -1))
            iteration(None, QUADS - 1)

        @block.sync
        def _(sp):
            nonlocal n_c, n_w
            x_q = A["x"].rearrange("s (h p) f -> p (s h) f", p=P)

            def load_x(q):
                src = x_q[:, bass.ds(q[0] * 8 + 8 * q[1], 8) if isinstance(q, tuple) else slice(8 * q, 8 * q + 8), :]
                sp.dma_start(xin[:], src).then_inc(S["x_loaded"], 16)

            load_x(0)
            first = [(eye[:], eye_d), (wconv[:], A["tok_W_k"].rearrange("(f d) k -> d f k", f=TAPS)),
                     (filt[:], A["tok_filt"].rearrange("f d -> d f"))]
            first += [(vec[dup[a], 0:1], A["tok_b_k"].rearrange("(d o) -> d o", o=1)) for a in range(2)]
            for dst, src in first:
                sp.dma_start(dst, src, allow_slow_non_contiguous=True).then_inc(c_loaded, 16)
            n_c = 16 * len(first)
            loads = [(masks[:], masks_d.rearrange("p (m t) -> p m t", t=P)), (keep[:], keep_d), (small[:], small_d),
                     (w_g2[:], A["attn_B_g"]),
                     (w_down[:], A["ffn_W2"].rearrange("e h d -> h e d")), (b_up[:], A["ffn_b1"].rearrange("e h -> h e"))]
            for a in range(2):
                loads += [
                    (w_g1[dup[a], :], A["attn_A_g"]),
                    (w_up[dup[a], :, :], A["ffn_W1"].rearrange("e d h -> d e h")),
                    (router_b[:, 8 * a:8 * a + 8], A["ffn_br"].rearrange("(o e) -> o e", o=1).broadcast_to([P, EXPERTS])),
                    (vec[dup[a], MIX:MIX + 6], A["attn_x_mix"].rearrange("m d -> d m")),
                ]
                for k, n in enumerate(("attn_b_w", "attn_b_a", "attn_k_k", "attn_k_a",
                                       "attn_gn_w", "attn_gn_b", "ffn_gamma", "ffn_beta")):
                    loads.append((vec[dup[a], k + 1:k + 2], A[n].rearrange("(d o) -> d o", o=1)))
            blocks = []
            for a in range(2):
                for k, n in enumerate(("W_r", "W_k", "W_v", "A_a", "B_a", "A_w", "B_w", "W_o")):
                    blocks.append((bd[dup[a], k, dup[a]], A["attn_" + n]))
                blocks += [
                    (rk_col[dup[a], a:a + 1], A["attn_r_k"].rearrange("(d o) -> d o", o=1)),
                    (w_router[dup[a], 8 * a:8 * a + 8], A["ffn_Wr"]),
                ]
                for part in range(3):
                    blocks.append((b_down[32 * part + 8 * a:32 * part + 8 * a + 8, dup[a]], A["ffn_b2"]))
            n_w = 16 * (len(loads) + len(blocks))
            for dst, src in loads:
                sp.dma_start(dst, src, allow_slow_non_contiguous=True).then_inc(w_loaded, 16)
            sp.wait_ge(w_zeroed, 1)
            for dst, src in blocks:
                sp.dma_start(dst, src, allow_slow_non_contiguous=True).then_inc(w_loaded, 16)

            def iteration(qa, qb):
                if qa is not None:
                    last = not isinstance(qa, tuple) and qa == QUADS - 1
                    if not last:
                        sp.wait_ge(S["x_turned"], nth(qa, "x_turned"))
                        load_x((qa[0], qa[1] + 1) if isinstance(qa, tuple) else qa + 1)
                if qb is not None:
                    sp.wait_ge(S["out_ready"], nth(qb, "out_ready"))
                    yv = y[:].rearrange("p (c a d) -> p c a d", c=NCH, a=2)
                    for b in range(2):
                        for a in range(2):
                            s = 2 * a + b
                            row = (bass.ds(qb[0] * QUAD + (qb[1] * QUAD + s), 1) if isinstance(qb, tuple)
                                   else slice(QUAD * qb + s, QUAD * qb + s + 1))
                            sp.dma_start(out[row, :, :].rearrange("s (c t) d -> t (s c) d", c=NCH),
                                         yv[b * HALF:b * HALF + CHUNK, :, a, :]).then_inc(S["y_stored"], 16)

            iteration(0, None)
            iteration(1, 0)
            if QUADS > 3:
                with sp.Fori(2, QUADS - 1) as i:
                    iteration((i, 0), (i, -1))
            if QUADS > 2:
                iteration(QUADS - 1, QUADS - 2)
            iteration(None, QUADS - 1)
            sp.wait_ge(S["y_stored"], nth(QUADS - 1, "y_stored"))

        @block.gpsimd
        def _(pool):
            for tile in (bd[:], rk_col[:], w_router[:], b_down[:], delta[:], hT[:], state[:], state_d[:], gate_parts[:]):
                last = nc.gpsimd.memset(tile, 0.0)
            last.then_inc(w_zeroed, 1)
            pool.wait_ge(w_loaded, n_w)

            def rsqrt(q, st, src, dst, ready, done):
                pool.wait_ge(S[ready], nth(q, ready))
                nc.gpsimd.tensor_tensor(st[:, dst, :], st[:, src, :], minus_half, ALU.pow).then_inc(S[done], 1)

            def iteration(qa, qb):
                if qb is not None:
                    rsqrt(qb, st_g, 2, 3, "gn_var", "gn_rstd")
                if qa is not None:
                    rsqrt(qa, st1, 2, 3, "ln1_var", "ln1_rstd")
                if qb is not None:
                    rsqrt(qb, st2, 2, 3, "ln2_var", "ln2_rstd")
                    rsqrt(qb, st2, 6, 7, "ln2_var2", "ln2_rstd2")
                if qa is not None:
                    rsqrt(qa, st_k, 0, 1, "kk_max", "kk_inv")
                    for g in range(2):
                        pool.wait_ge(S["masked"], nth(qa, "masked", 8 * g + 5))
                        nc.gpsimd.tensor_tensor(group(NT, g), group(NT, g), four(eye[:]), ALU.add).then_inc(S["eye_added"], 1)
                        pool.wait_ge(S["eye_added"], nth(qa, "eye_added", g + 1))
                        nc.gpsimd.tensor_tensor(group(XT, g), group(NT, g), four(masks[:, 2, :]),
                                                ALU.mult).then_inc(S["xt_first"], 1)

            pipeline(pool, iteration)

        @block.tensor
        def _(pe):
            mm = nc.tensor.matmul

            def turn(dst, src, done):
                for c in range(NCH):
                    last = nc.tensor.transpose(dst[:, c * P:(c + 1) * P], src[:, c * P:(c + 1) * P], eye[:])
                last.then_inc(S[done], 1)

            def chunk_b(c, b):
                return slice(c * P + b * HALF, c * P + b * HALF + HALF)

            def turn_x(q):
                pe.wait_ge(S["x_loaded"], nth(q, "x_loaded"))
                if later(q):
                    pe.wait_ge(S["o_ready"], nth(before(q), "o_ready"))
                for h in range(2):
                    for s in range(QUAD):
                        last = nc.tensor.transpose(bank[h][:, s * P:(s + 1) * P], xin[:, 4 * h + s, :], eye[:])
                    last.then_inc(S["x_turned"], 1)

            def conv(q, b):
                if b == 0:
                    pe.wait_ge(S["xT_ready_v"], nth(q, "xT_ready_v"))
                    pe.wait_ge(S["xT_ready_s"], nth(q, "xT_ready_s"))
                    if later(q):
                        pe.wait_ge(S["st_ready"], nth(before(q), "st_ready"))
                for f in range(TAPS):
                    for a in range(2):
                        last = mm(bank[2 + b][dup[a], 0:T], wconv[:, f, :], xT[:, 2 * a + b, f:f + T],
                                  start=(f == 0), stop=(f == TAPS - 1))
                last.then_inc(S["conv_done"], 1)

            def turn_h(q):
                pe.wait_ge(S["h_ready"], nth(q, "h_ready"))
                turn(bank[0], hT, "h_turned")

            def turn_x1(q):
                pe.wait_ge(S["ln1_done"], nth(q, "ln1_done"))
                turn(bank[1], x1_tm, "x1_turned")

            def project(q, m, ready, w, bk, done, free=None):
                if free:
                    pe.wait_ge(S[free], nth(q, free))
                pe.wait_ge(S["mixed"], nth(q, "mixed", ready))
                mm(bank[bk][:], bd[:, w, :], xm[:, m, :], start=True, stop=True).then_inc(S[done], 1)

            def projections_1(q):
                project(q, M_W, 1, W_W1, 2, "w_proj")
                project(q, M_A, 2, W_A1, 3, "a_proj")
                project(q, M_K, 3, W_K, 0, "k_proj")
                project(q, M_R, 4, W_R, 1, "r_proj")

            def projections_2(q):
                pe.wait_ge(S["w_act"], nth(q, "w_act", 1))
                mm(bank[2][:], bd[:, W_W2, :], low_w[:], start=True, stop=True).then_inc(S["w_proj"], 1)
                pe.wait_ge(S["a_act"], nth(q, "a_act", 1))
                mm(bank[3][:], bd[:, W_A2, :], low_a[:], start=True, stop=True).then_inc(S["a_proj"], 1)
                pe.wait_ge(S["kk_sq"], nth(q, "kk_sq"))
                pe.wait_ge(S["k_act"], nth(q, "k_act"))
                for c in range(NCH):
                    last = mm(bank[0][:, 2 * c:2 * c + 2], kk2[:, c * P:(c + 1) * P], half_ones, start=True, stop=True)
                last.then_inc(S["kk_norm"], 1)
                pe.wait_ge(S["r_act"], nth(q, "r_act"))
                pe.wait_ge(S["mixed"], nth(q, "mixed", 5))
                for c in range(NCH):
                    last = mm(bank[1][:, c * P:(c + 1) * P], xm[:, M_V, c * P:(c + 1) * P], bd[:, W_V, :],
                              start=True, stop=True)
                last.then_inc(S["v_proj"], 1)
                pe.wait_ge(S["w_act"], nth(q, "w_act", 2))
                pe.wait_ge(S["mixed"], nth(q, "mixed", 6))
                mm(bank[2][:], w_g1[dup[0], :], xm[dup[0], M_G, :], start=True, stop=True).then_inc(S["g_proj"], 1)
                pe.wait_ge(S["a_act"], nth(q, "a_act", 2))
                mm(bank[3][:], w_g1[dup[1], :], xm[dup[1], M_G, :], start=True, stop=True).then_inc(S["g_proj"], 1)
                pe.wait_ge(S["v_act"], nth(q, "v_act"))
                pe.wait_ge(S["g_act"], nth(q, "g_act", 2))
                for a in range(2):
                    last = mm(bank[1][dup[a], :], w_g2[:], sig_g[:, a, :], start=True, stop=True)
                last.then_inc(S["g_proj"], 1)
                pe.wait_ge(S["kk_bc"], nth(q, "kk_bc"))
                turn(bank[0], inv_b, "kk_turned")

            def hats(q):
                pe.wait_ge(S["g_act"], nth(q, "g_act"))
                pe.wait_ge(S["prep"], nth(q, "prep", 9))
                turn(bank[1], bh, "hats_turned")
                pe.wait_ge(S["prep"], nth(q, "prep", 10))
                turn(bank[3], kh, "hats_turned")

            def scores(q, c):
                if c < 2:
                    pe.wait_ge(S["hats_ready"], nth(q, "hats_ready", c + 1))
                else:
                    pe.wait_ge(S["masked"], nth(q, "masked", 4 * (c - 1)))
                cols = slice(c * P, (c + 1) * P)
                for a in range(2):
                    for key, src in enumerate((bt, kt)):
                        last = mm(bank[2 * (c % 2) + a][:, 256 * key:256 * key + 256].rearrange("p (r t) -> p r t", r=2),
                                  src[dup[a], cols], ar[dup[a], :, cols], start=True, stop=True)
                last.then_inc(S["scores_done"], 1)

            def x_first(q, g):
                pe.wait_ge(S["xt_first"], nth(q, "xt_first", g + 1))
                pe.wait_ge(S["masked"], nth(q, "masked", 12))
                for u in range(4):
                    last = nc.tensor.transpose(bank[g][:, u * P:(u + 1) * P], XT[:, 2 * g + u // 2, u % 2, :], eye[:])
                last.then_inc(S["x_first"], 1)

            def level_y(q, lvl, g):
                if lvl == 0:
                    pe.wait_ge(S["masked"], nth(q, "masked"))
                    pe.wait_ge(S["x_first_ready"], nth(q, "x_first_ready", g + 1))
                else:
                    pe.wait_ge(S["z_ready"], nth(q, "z_ready", 2 * (lvl - 1) + g + 1))
                for u in range(4):
                    c, a = 2 * g + u // 2, u % 2
                    last = mm(bank[2 + g][:, u * P:(u + 1) * P], NT[:, c, a, :], X[:, c, a, :], start=True, stop=True)
                last.then_inc(S["y_done"], 1)

            def level_z(q, lvl, g):
                pe.wait_ge(S["y_ready"], nth(q, "y_ready", 2 * lvl + g + 1))
                if lvl > 0:
                    pe.wait_ge(S["zt_ready"], nth(q, "zt_ready", 2 * (lvl - 1) + g + 1))
                w, m = (XT, Y) if lvl < LEVELS - 1 else (Y, XT)
                for u in range(4):
                    c, a = 2 * g + u // 2, u % 2
                    last = mm(bank[g][:, u * P:(u + 1) * P], w[:, c, a, :], m[:, c, a, :], start=True, stop=True)
                last.then_inc(S["z_done"], 1)

            def level_t(q, lvl, g):
                pe.wait_ge(S["z_ready"], nth(q, "z_ready", 2 * lvl + g + 1))
                for u in range(4):
                    last = nc.tensor.transpose(bank[g][:, u * P:(u + 1) * P], X[:, 2 * g + u // 2, u % 2, :], eye[:])
                last.then_inc(S["zt_done"], 1)

            def value(c, a):
                return v_tm[:, c * P + a * D:c * P + a * D + D]

            def chunk_r(q, c):
                if c == 0:
                    pe.wait_ge(S["z_ready"], nth(q, "z_ready"))
                else:
                    pe.wait_ge(S["sa_ready"], nth(q, "sa_ready", c))
                    pe.wait_ge(S["st_ready"], nth(q, "st_ready", 2 * c))
                for a in range(2):
                    last = mm(bank[0][:, a * D:a * D + D], AK[:, c, a, :], value(c, a), start=(a == 0),
                              stop=(c == 0), skip_group_check=True)
                if c > 0:
                    for b in range(2):
                        last = mm(bank[0][dup[b], 0:P], ar[:, 0, chunk_b(c, b)], state[:, b, :], start=False, stop=True,
                                  skip_group_check=True)
                last.then_inc(S["r_done"], 1)

            def chunk_sa(q, c):
                pe.wait_ge(S["r_ready"], nth(q, "r_ready", c + 1))
                for a in range(2):
                    last = mm(bank[0][:, P + a * D:P + a * D + D], XT[:, c, a, :], r_sb[:, a * D:a * D + D],
                              start=True, stop=True)
                last.then_inc(S["sa_done"], 1)

            def chunk_bonus(q):
                pe.wait_ge(S["rk_ready"], nth(q, "rk_ready"))
                for c in range(NCH):
                    last = mm(bank[3][:, 2 * c:2 * c + 2], rk[:, c * P:(c + 1) * P], rk_col[:], start=True, stop=True)
                last.then_inc(S["bonus_done"], 1)

            def chunk_o1(q, c):
                if c == 0:
                    pe.wait_ge(S["bonus_ready"], nth(q, "bonus_ready"))
                o0 = c * P
                for a in range(2):
                    mm(bank[1][:, o0 + a * D:o0 + a * D + D], RK[:, c, a, :], value(c, a), start=(a == 0), stop=False,
                       skip_group_check=True)
                if c > 0:
                    for b in range(2):
                        mm(bank[1][dup[b], o0:o0 + P], ar[:, 1, chunk_b(c, b)], state[:, b, :], start=False, stop=False,
                           skip_group_check=True)

            def chunk_o2(q, c):
                pe.wait_ge(S["sa_ready"], nth(q, "sa_ready", c + 1))
                o0 = c * P
                for a in range(2):
                    last = mm(bank[1][:, o0 + a * D:o0 + a * D + D], RB[:, c, a, :], sa[:, a * D:a * D + D],
                              start=False, stop=True, skip_group_check=True)
                if c == NCH - 1:
                    last.then_inc(S["o_done"], 1)

            def chunk_state(q, c):
                for b in range(2):
                    for a in range(2):
                        cols = slice(c * P + a * D, c * P + a * D + D)
                        st = bank[2 + b][dup[a], 0:D]
                        mm(st, bh_tm[dup[b], cols], sa[dup[b], a * D:a * D + D], start=True, stop=False)
                        last = mm(st, kh_tm[dup[b], cols], v_tm[dup[b], cols], start=False, stop=True)
                last.then_inc(S["st_done"], 1)

            def head_norm(q):
                pe.wait_ge(S["gn_done"], nth(q, "gn_done"))
                if later(q):
                    pe.wait_ge(S["out_ready"], nth(before(q), "out_ready"))
                turn(bank[4], cent_g, "on_turned")
                pe.wait_ge(S["bv_ready"], nth(q, "bv_ready"))
                turn(bank[5], bv, "bv_turned")

            def out_proj(q):
                pe.wait_ge(S["og_ready"], nth(q, "og_ready"))
                for c in range(NCH):
                    last = mm(bank[6][:, c * P:(c + 1) * P], ogT[:, c * P:(c + 1) * P], bd[:, W_O, :], start=True, stop=True)
                last.then_inc(S["att_done"], 1)

            def turn_xn(q):
                pe.wait_ge(S["ln2_done"], nth(q, "ln2_done"))
                turn(bank[7], cent2, "xn_turned")

            def router(q):
                pe.wait_ge(S["xn_ready"], nth(q, "xn_ready"))
                for c in range(NCH):
                    last = mm(bank[4][:, 16 * c:16 * c + 16], xnT[:, c * P:(c + 1) * P], w_router[:], start=True, stop=True)
                last.then_inc(S["router_done"], 1)

            def gates(q):
                pe.wait_ge(S["top"], nth(q, "top"))
                half = bank[5].bitcast(BF16)
                for c in range(NCH):
                    last = nc.tensor.transpose(half[:, c * P:(c + 1) * P], gate_parts[:, c, :], eye_h[:])
                last.then_inc(S["gates_turned"], 1)

            def bias_down(q):
                pe.wait_ge(S["gatesT_ready"], nth(q, "gatesT_ready"))
                for part in range(3):
                    mm(bank[7][:], b_parts[:, part, :], gateT[:], start=(part == 0), stop=False, skip_group_check=True)

            def expert_slot(q, n):
                if n < 2 * EXPERTS:
                    e, a = n // 2, n % 2
                    if n >= 2:
                        pe.wait_ge(S["act_done"], nth(q, "act_done", n - 1))
                    mm(bank[4 + a][:], w_up[dup[a], e, :], xnT[dup[a], :], start=True, stop=True).then_inc(S["up_done"], 1)
                if 1 <= n <= 2 * EXPERTS:
                    if n >= 2:
                        pe.wait_ge(S["weighted"], nth(q, "weighted", n - 1))
                    mm(bank[6][:], spread[:, n - 1, :], gateT[:], start=True, stop=True).then_inc(S["spread_done"], 1)
                if n % 2 == 1 and n >= 3:
                    e = (n - 3) // 2
                    pe.wait_ge(S["weighted"], nth(q, "weighted", 2 * e + 2))
                    for a in range(2):
                        last = mm(bank[7][dup[a], :], w_down[:, e, :], hidw[:, a, :], start=False, stop=(e == EXPERTS - 1),
                                  skip_group_check=True)
                    last.then_inc(S["down_done"], 1)

            def turn_ffn(q):
                pe.wait_ge(S["ffn_ready"], nth(q, "ffn_ready"))
                turn(bank[4], ffnT, "ffn_turned")

            def iteration(qa, qb):
                on_a, on_b = qa is not None, qb is not None
                slots = iter(range(SLOTS))

                def experts(n=1):
                    for _ in range(n if on_b else 0):
                        expert_slot(qb, next(slots))

                if on_a:
                    turn_x(qa)
                    conv(qa, 0)
                if on_b:
                    head_norm(qb)
                if on_a:
                    conv(qa, 1)
                if on_b:
                    out_proj(qb)
                if on_a:
                    turn_h(qa)
                    turn_x1(qa)
                    projections_1(qa)
                if on_b:
                    turn_xn(qb)
                if on_a:
                    projections_2(qa)
                if on_b:
                    router(qb)
                if on_a:
                    hats(qa)
                    for c in range(NCH):
                        scores(qa, c)
                if on_b:
                    gates(qb)
                    bias_down(qb)
                if on_a:
                    x_first(qa, 0)
                experts()
                if on_a:
                    x_first(qa, 1)
                for lvl in range(LEVELS):
                    if on_a:
                        level_y(qa, lvl, 0)
                        level_y(qa, lvl, 1)
                    experts()
                    if on_a:
                        level_z(qa, lvl, 0)
                        level_z(qa, lvl, 1)
                        if lvl < LEVELS - 1:
                            level_t(qa, lvl, 0)
                            level_t(qa, lvl, 1)
                if on_a:
                    chunk_bonus(qa)
                for c in range(NCH):
                    if on_a:
                        chunk_r(qa, c)
                    experts(2 if c == NCH - 1 else 1)
                    if on_a:
                        chunk_sa(qa, c)
                        chunk_o1(qa, c)
                    experts()
                    if on_a:
                        chunk_o2(qa, c)
                        if c < NCH - 1:
                            chunk_state(qa, c)
                    if c < NCH - 1:
                        experts()
                if on_b:
                    turn_ffn(qb)

            pe.wait_ge(w_built, 1)
            pe.wait_ge(c_loaded, n_c)
            pe.wait_ge(w_loaded, n_w)
            pe.wait_ge(w_built, 6)
            pipeline(pe, iteration)

        @block.scalar
        def _(act):
            copy, activation = nc.scalar.copy, nc.scalar.activation

            def v(k):
                return vec[:, k:k + 1]

            def square(q, dst, src, name):
                act.wait_ge(S[name + "_cent"], nth(q, name + "_cent"))
                activation(dst[:], src[:], ACT.Square).then_inc(S[name + "_sq"], 1)

            def move_x(q):
                act.wait_ge(S["x_turned"], nth(q, "x_turned", 2))
                copy(xT[:, 2:4, :].rearrange("p s t -> p (s t)"), bank[1][:]).then_inc(S["xT_ready_s"], 1)

            def tokens(q, b):
                act.wait_ge(S["conv_done"], nth(q, "conv_done", b + 1))
                activation(fm(hT[:])[:, :, b, 0:CHUNK], bank[2 + b][:, 0:T].rearrange("p (c t) -> p c t", c=NCH),
                           ACT.Relu, bias=v(B_CONV)).then_inc(S["h_ready"], 1)

            def move_h(q, qb):
                act.wait_ge(S["h_turned"], nth(q, "h_turned"))
                if qb is not None:
                    act.wait_ge(S["h2_ready"], nth(qb, "h2_ready"))
                copy(h_tm[:], bank[0][:]).then_inc(S["htm_ready"], 1)

            def move_x1(q):
                act.wait_ge(S["x1_turned"], nth(q, "x1_turned"))
                copy(x1T[:], bank[1][:]).then_inc(S["x1T_ready"], 1)

            def projected_1(q):
                act.wait_ge(S["w_proj"], nth(q, "w_proj", 1))
                activation(low_w[:], bank[2][:], ACT.Tanh).then_inc(S["w_act"], 1)
                act.wait_ge(S["a_proj"], nth(q, "a_proj", 1))
                copy(low_a[:], bank[3][:]).then_inc(S["a_act"], 1)
                act.wait_ge(S["k_proj"], nth(q, "k_proj"))
                activation(kk2[:], bank[0][:], ACT.Square, scale=v(K_K)).then_inc(S["kk_sq"], 1)
                copy(kT[:], bank[0][:]).then_inc(S["k_act"], 1)
                act.wait_ge(S["r_proj"], nth(q, "r_proj"))
                copy(rT[:], bank[1][:]).then_inc(S["r_act"], 1)

            def projected_2(q, qb):
                act.wait_ge(S["w_proj"], nth(q, "w_proj", 2))
                activation(sig_w[:], bank[2][:], ACT.Sigmoid, bias=v(B_W)).then_inc(S["w_act"], 1)
                act.wait_ge(S["a_proj"], nth(q, "a_proj", 2))
                activation(aT[:], bank[3][:], ACT.Sigmoid, bias=v(B_A)).then_inc(S["a_act"], 1)
                act.wait_ge(S["v_proj"], nth(q, "v_proj"))
                if qb is not None:
                    act.wait_ge(S["og_ready"], nth(qb, "og_ready"))
                copy(v_tm[:], bank[1][:]).then_inc(S["v_act"], 1)
                for a in range(2):
                    act.wait_ge(S["g_proj"], nth(q, "g_proj", a + 1))
                    activation(sig_g[:, a, :], bank[2 + a][:], ACT.Sigmoid).then_inc(S["g_act"], 1)
                act.wait_ge(S["g_proj"], nth(q, "g_proj", 3))
                copy(gT[:], bank[1][:]).then_inc(S["g_act"], 1)

            def decays(q):
                act.wait_ge(S["cum_done"], nth(q, "cum_done"))
                activation(e_neg[:], cum[:], ACT.Exp, scale=-DECAY_SCALE).then_inc(S["exps"], 1)
                act.wait_ge(S["cumx_done"], nth(q, "cumx_done"))
                activation(e_ex[:], cumx[:], ACT.Exp, scale=DECAY_SCALE).then_inc(S["exps"], 1)
                activation(e_in[:], cum[:], ACT.Exp, scale=DECAY_SCALE).then_inc(S["exps"], 1)

            def move_hats(q):
                act.wait_ge(S["hats_turned"], nth(q, "hats_turned", 1))
                copy(bh_tm[:], bank[1][:]).then_inc(S["hats_ready"], 1)
                act.wait_ge(S["hats_turned"], nth(q, "hats_turned", 2))
                copy(kh_tm[:], bank[3][:]).then_inc(S["hats_ready"], 1)

            def move_first(q, g):
                act.wait_ge(S["x_first"], nth(q, "x_first", g + 1))
                copy(group(X, g), grp(bank[g][:], 4)).then_inc(S["x_first_ready"], 1)

            def move_z(q, lvl, g):
                act.wait_ge(S["z_done"], nth(q, "z_done", 2 * lvl + g + 1))
                copy(group(X if lvl < LEVELS - 1 else XT, g), grp(bank[g][:], 4)).then_inc(S["z_ready"], 1)

            def move_t(q, lvl, g):
                act.wait_ge(S["zt_done"], nth(q, "zt_done", 2 * lvl + g + 1))
                copy(group(XT, g), grp(bank[g][:], 4)).then_inc(S["zt_ready"], 1)

            def move_r(q, c):
                act.wait_ge(S["r_done"], nth(q, "r_done", c + 1))
                copy(r_sb[:], bank[0][:, 0:P]).then_inc(S["r_ready"], 1)

            def move_o(q):
                act.wait_ge(S["o_done"], nth(q, "o_done"))
                copy(o_tm[:], bank[1][:]).then_inc(S["o_ready"], 1)

            def head_affine(q):
                act.wait_ge(S["on_turned"], nth(q, "on_turned"))
                activation(onT[:], bank[4][:], ACT.Identity, scale=v(GN_W), bias=v(GN_B)).then_inc(S["on_ready"], 1)

            def ffn_affine(q):
                act.wait_ge(S["xn_turned"], nth(q, "xn_turned"))
                activation(xnT[:], bank[7][:], ACT.Identity, scale=v(GAMMA), bias=v(BETA)).then_inc(S["xn_ready"], 1)

            def gate_tanh(q):
                act.wait_ge(S["top"], nth(q, "top", 13))
                activation(tops[:, 6, :, 0], tops[:, 5, :, 0], ACT.Tanh, scale=0.5).then_inc(S["gate_tanh"], 1)

            def move_gates(q):
                act.wait_ge(S["gates_turned"], nth(q, "gates_turned"))
                copy(gateT[:], bank[5].bitcast(BF16)[:, 0:COLS]).then_inc(S["gatesT_ready"], 1)

            def expert_slot(q, n):
                if n < 2 * EXPERTS:
                    e, a = n // 2, n % 2
                    act.wait_ge(S["up_done"], nth(q, "up_done", n + 1))
                    if n >= 2:
                        act.wait_ge(S["weighted"], nth(q, "weighted", n - 1))
                    activation(hid[:, a, :], bank[4 + a][:], ACT.Gelu, bias=b_up[:, e:e + 1]).then_inc(S["act_done"], 1)

            def move_ffn(q):
                act.wait_ge(S["down_done"], nth(q, "down_done"))
                copy(ffnT[:], bank[7][:]).then_inc(S["ffn_ready"], 1)

            def iteration(qa, qb):
                on_a, on_b = qa is not None, qb is not None
                slots = iter(range(SLOTS))

                def experts(n=1):
                    for _ in range(n if on_b else 0):
                        expert_slot(qb, next(slots))

                if on_a:
                    move_x(qa)
                if on_b:
                    square(qb, sq_g, cent_g, "gn")
                if on_a:
                    tokens(qa, 0)
                if on_b:
                    head_affine(qb)
                if on_a:
                    tokens(qa, 1)
                    move_h(qa, qb)
                    square(qa, sq1, cent1, "ln1")
                if on_b:
                    square(qb, sq2, cent2, "ln2")
                if on_a:
                    move_x1(qa)
                    projected_1(qa)
                if on_b:
                    ffn_affine(qb)
                if on_a:
                    projected_2(qa, qb)
                    decays(qa)
                if on_b:
                    gate_tanh(qb)
                if on_a:
                    move_hats(qa)
                if on_b:
                    move_gates(qb)
                if on_a:
                    move_first(qa, 0)
                experts()
                if on_a:
                    move_first(qa, 1)
                for lvl in range(LEVELS):
                    experts()
                    if on_a:
                        move_z(qa, lvl, 0)
                        move_z(qa, lvl, 1)
                        if lvl < LEVELS - 1:
                            move_t(qa, lvl, 0)
                            move_t(qa, lvl, 1)
                for c in range(NCH):
                    if on_a:
                        move_r(qa, c)
                    experts(2 if c == NCH - 1 else 1)
                    experts()
                    if c < NCH - 1:
                        experts()
                if on_b:
                    move_ffn(qb)
                if on_a:
                    move_o(qa)

            act.wait_ge(c_loaded, n_c)
            act.wait_ge(w_zeroed, 1)
            act.wait_ge(w_loaded, n_w)
            pipeline(act, iteration)

        @block.vector
        def _(dve):
            tt, ts, stt = nc.vector.tensor_tensor, nc.vector.tensor_scalar, nc.vector.scalar_tensor_tensor

            def v(k):
                return vec[:, k:k + 1]

            def centre(q, src, cent, st, name, ready):
                dve.wait_ge(S[ready], nth(q, ready))
                nc.vector.reduce_sum(st[:, 0, :], grp(src[:]), AX_X).then_inc(S[name + "_sum"], 1)
                dve.wait_ge(S[name + "_sum"], nth(q, name + "_sum"))
                ts(st[:, 1, :], st[:, 0, :], -1.0 / D, None, ALU.mult).then_inc(S[name + "_mean"], 1)
                dve.wait_ge(S[name + "_mean"], nth(q, name + "_mean"))
                tt(grp(cent[:]), grp(src[:]), wide(st[:, 1, :]), ALU.add).then_inc(S[name + "_cent"], 1)

            def variance(q, sq, st, name, eps):
                dve.wait_ge(S[name + "_sq"], nth(q, name + "_sq"))
                nc.vector.reduce_sum(st[:, 0, :], grp(sq[:]), AX_X).then_inc(S[name + "_ss"], 1)
                dve.wait_ge(S[name + "_ss"], nth(q, name + "_ss"))
                ts(st[:, 2, :], st[:, 0, :], 1.0 / D, eps, ALU.mult, ALU.add).then_inc(S[name + "_var"], 1)

            def move_x(q):
                dve.wait_ge(S["x_turned"], nth(q, "x_turned", 1))
                nc.vector.tensor_copy(xT[:, 0:2, :].rearrange("p s t -> p (s t)"), bank[0][:]).then_inc(S["xT_ready_v"], 1)

            def mixes(q):
                dve.wait_ge(S["x1T_ready"], nth(q, "x1T_ready"))
                xv, dv = fm(x1T[:]), fm(delta[:])
                tt(dv[:, :, :, 1:CHUNK], xv[:, :, :, 0:CHUNK - 1], xv[:, :, :, 1:CHUNK], ALU.subtract).then_inc(S["delta_ready"], 1)
                tt(dv[:, 1:NCH, :, 0], xv[:, 0:NCH - 1, :, CHUNK - 1], xv[:, 1:NCH, :, 0], ALU.subtract).then_inc(S["delta_ready"], 1)
                ts(dv[:, 0, :, 0], xv[:, 0, :, 0], -1.0, None, ALU.mult).then_inc(S["delta_ready"], 1)
                dve.wait_ge(S["delta_ready"], nth(q, "delta_ready"))
                for m in (M_W, M_A, M_K, M_R, M_V, M_G):
                    stt(xm[:, m, :], delta[:], v(MIX + m), x1T[:], ALU.mult, ALU.add).then_inc(S["mixed"], 1)

            def decay_sums(q):
                dve.wait_ge(S["kk_norm"], nth(q, "kk_norm"))
                ts(st_k[:, 0, :], bank[0][:, 0:8], 1e-24, None, ALU.max).then_inc(S["kk_max"], 1)
                dve.wait_ge(S["w_act"], nth(q, "w_act", 2))
                nc.vector.tensor_tensor_scan(cum[:], keep[:], sig_w[:], 0.0, ALU.mult, ALU.add).then_inc(S["cum_done"], 1)
                dve.wait_ge(S["cum_done"], nth(q, "cum_done"))
                tt(cumx[:], cum[:], sig_w[:], ALU.subtract).then_inc(S["cumx_done"], 1)
                dve.wait_ge(S["kk_inv"], nth(q, "kk_inv"))
                nc.vector.tensor_copy(grp(inv_b[:]), wide(st_k[:, 1, :])).then_inc(S["kk_bc"], 1)

            def prepare(q):
                dve.wait_ge(S["a_act"], nth(q, "a_act", 2))
                ts(t1[:], aT[:], 1.0, v(K_A), ALU.subtract, ALU.mult).then_inc(S["prep"], 1)
                dve.wait_ge(S["prep"], nth(q, "prep", 1))
                dve.wait_ge(S["k_act"], nth(q, "k_act"))
                stt(k2[:], t1[:], 1.0, kT[:], ALU.add, ALU.mult).then_inc(S["prep"], 1)
                dve.wait_ge(S["kk_turned"], nth(q, "kk_turned"))
                stt(kkn[:], kT[:], v(K_K), bank[0][:], ALU.mult, ALU.mult).then_inc(S["prep"], 1)
                dve.wait_ge(S["prep"], nth(q, "prep", 3))
                tt(ka[:], kkn[:], aT[:], ALU.mult).then_inc(S["prep"], 1)
                dve.wait_ge(S["exps"], nth(q, "exps"))
                tt(kt[:], k2[:], e_neg[:], ALU.mult).then_inc(S["prep"], 1)
                dve.wait_ge(S["prep"], nth(q, "prep", 5))
                tt(bt[:], ka[:], e_neg[:], ALU.mult).then_inc(S["prep"], 1)
                stt(ar[:, 0, :], kkn[:], -1.0, e_ex[:], ALU.mult, ALU.mult).then_inc(S["prep"], 1)
                dve.wait_ge(S["r_act"], nth(q, "r_act"))
                tt(ar[:, 1, :], rT[:], e_in[:], ALU.mult).then_inc(S["prep"], 1)
                dve.wait_ge(S["prep"], nth(q, "prep", 6))
                last_decay = fm(e_in[:])[:, :, :, CHUNK - 1].rearrange("p c b -> p (c b)")
                tt(grp(bh[:]), grp(bt[:]), wide(last_decay), ALU.mult).then_inc(S["prep"], 1)
                tt(grp(kh[:]), grp(kt[:]), wide(last_decay), ALU.mult).then_inc(S["prep"], 1)
                tt(rk[:], rT[:], k2[:], ALU.mult).then_inc(S["rk_ready"], 1)

            def mask(q, c):
                dve.wait_ge(S["scores_done"], nth(q, "scores_done", c + 1))
                both = psum[:, 2 * (c % 2):2 * (c % 2) + 2, :].rearrange("p a (k r t) -> p a k r t", k=2, r=2)
                for key, r, dst in ((0, 0, NT), (0, 1, RB), (1, 0, AK), (1, 1, RK)):
                    tt(dst[:, c, :, :], both[:, :, key, r, :], masks[:, r, :].unsqueeze(1).broadcast_to([P, 2, P]),
                       ALU.mult).then_inc(S["masked"], 1)

            def mask_y(q, lvl, g):
                dve.wait_ge(S["y_done"], nth(q, "y_done", 2 * lvl + g + 1))
                tt(group(Y, g), grp(bank[2 + g][:], 4), four(masks[:, 3 + lvl, :]), ALU.mult).then_inc(S["y_ready"], 1)

            def move_bonus(q):
                dve.wait_ge(S["bonus_done"], nth(q, "bonus_done"))
                nc.vector.tensor_copy(bonus[:], bank[3][:, 0:8]).then_inc(S["bonus_ready"], 1)

            def move_sa(q, c):
                dve.wait_ge(S["sa_done"], nth(q, "sa_done", c + 1))
                nc.vector.tensor_copy(sa[:], bank[0][:, P:2 * P]).then_inc(S["sa_ready"], 1)

            def new_state(q, c):
                dve.wait_ge(S["st_done"], nth(q, "st_done", c + 1))
                if c > 0:
                    dve.wait_ge(S["decayed"], nth(q, "decayed", c))
                for a in range(2):
                    new = psum[dup[a], 2:4, 0:D]
                    if c == 0:
                        nc.vector.tensor_copy(state[dup[a], :, dup[a]], new).then_inc(S["st_ready"], 1)
                    else:
                        tt(state[dup[a], :, dup[a]], state_d[dup[a], :, dup[a]], new, ALU.add).then_inc(S["st_ready"], 1)
                if c < NCH - 2:
                    dve.wait_ge(S["st_ready"], nth(q, "st_ready", 2 * c + 2))
                    tt(state_d[:], state[:], wide(fm(e_in[:])[:, c + 1, :, CHUNK - 1], P), ALU.mult).then_inc(S["decayed"], 1)

            def head_norm(q):
                centre(q, o_tm, cent_g, st_g, "gn", "o_ready")
                tt(grp(bv[:]), grp(v_tm[:]), wide(bonus[:]), ALU.mult).then_inc(S["bv_ready"], 1)
                variance(q, sq_g, st_g, "gn", GN_EPS)
                dve.wait_ge(S["gn_rstd"], nth(q, "gn_rstd"))
                tt(grp(cent_g[:]), grp(cent_g[:]), wide(st_g[:, 3, :]), ALU.mult).then_inc(S["gn_done"], 1)

            def head_out(q):
                dve.wait_ge(S["bv_turned"], nth(q, "bv_turned"))
                dve.wait_ge(S["on_ready"], nth(q, "on_ready"))
                tt(onT[:], onT[:], bank[5][:], ALU.add).then_inc(S["og_sum"], 1)
                dve.wait_ge(S["og_sum"], nth(q, "og_sum"))
                tt(ogT[:], onT[:], gT[:], ALU.mult).then_inc(S["og_ready"], 1)
                dve.wait_ge(S["att_done"], nth(q, "att_done"))
                tt(h2[:], h_tm[:], bank[6][:], ALU.add).then_inc(S["h2_ready"], 1)

            def ln2_scale(q):
                dve.wait_ge(S["ln2_rstd"], nth(q, "ln2_rstd"))
                dve.wait_ge(S["ln2_ss"], nth(q, "ln2_ss"))
                ts(st2[:, 4, :], st2[:, 0, :], 1.0 / D, None, ALU.mult).then_inc(S["ln2_var0"], 1)
                tt(st2[:, 5, :], st2[:, 3, :], st2[:, 3, :], ALU.mult).then_inc(S["ln2_rr"], 1)
                dve.wait_ge(S["ln2_rr"], nth(q, "ln2_rr"))
                tt(st2[:, 8, :], st2[:, 4, :], st2[:, 5, :], ALU.mult).then_inc(S["ln2_ratio"], 1)
                dve.wait_ge(S["ln2_ratio"], nth(q, "ln2_ratio"))
                ts(st2[:, 6, :], st2[:, 8, :], LN_EPS, None, ALU.add).then_inc(S["ln2_var2"], 1)

            def ln2_finish(q):
                dve.wait_ge(S["ln2_rstd2"], nth(q, "ln2_rstd2"))
                tt(st2[:, 4, :], st2[:, 3, :], st2[:, 7, :], ALU.mult).then_inc(S["ln2_scale"], 1)
                dve.wait_ge(S["ln2_scale"], nth(q, "ln2_scale"))
                tt(grp(cent2[:]), grp(cent2[:]), wide(st2[:, 4, :]), ALU.mult).then_inc(S["ln2_done"], 1)

            L, EQ, EQ2, T1, T2, DIFF, TH, F1, F2, MX, L2, W1, W2 = (tops[:, k] for k in range(13))
            G = gate[:].rearrange("p c (a e) -> p (c a) e", a=2)
            ranks = rank.unsqueeze(1).broadcast_to([P, 8, EXPERTS])

            def one(t):
                return t[:, :, 0:1].broadcast_to([P, 8, EXPERTS])

            def step(q, k, instruction):
                instruction.then_inc(S["top"], 1)
                dve.wait_ge(S["top"], nth(q, "top", k))

            def top_experts(q):
                dve.wait_ge(S["router_done"], nth(q, "router_done"))
                step(q, 1, tt(L.rearrange("p (c a) e -> p c (a e)", a=2),
                             bank[4][:, 0:64].rearrange("p (c e) -> p c e", c=NCH),
                             router_b[:].unsqueeze(1).broadcast_to([P, NCH, 16]), ALU.add))
                step(q, 2, nc.vector.tensor_reduce(T1[:, :, 0], L, AX_X, ALU.max))
                step(q, 3, tt(EQ, L, one(T1), ALU.is_equal))
                step(q, 4, tt(EQ, EQ, ranks, ALU.mult))
                step(q, 5, nc.vector.tensor_reduce(MX[:, :, 0], EQ, AX_X, ALU.max))
                step(q, 6, tt(F1, EQ, one(MX), ALU.is_equal))
                step(q, 7, stt(L2, F1, -3e38, L, ALU.mult, ALU.add))
                step(q, 8, nc.vector.tensor_reduce(T2[:, :, 0], L2, AX_X, ALU.max))
                step(q, 9, tt(EQ2, L2, one(T2), ALU.is_equal))
                step(q, 10, tt(EQ2, EQ2, ranks, ALU.mult))
                step(q, 11, nc.vector.tensor_reduce(MX[:, :, 0], EQ2, AX_X, ALU.max))
                step(q, 12, tt(F2, EQ2, one(MX), ALU.is_equal))
                step(q, 13, tt(DIFF[:, :, 0], T2[:, :, 0], T1[:, :, 0], ALU.subtract))

            def top_gates(q):
                def part(k):
                    return gate_parts[:, :, 32 * k:32 * k + 16]

                dve.wait_ge(S["gate_tanh"], nth(q, "gate_tanh"))
                step(q, 14, ts(W1[:, :, 0], TH[:, :, 0], -0.5, 0.5, ALU.mult, ALU.add))
                step(q, 15, ts(W2[:, :, 0], TH[:, :, 0], 0.5, 0.5, ALU.mult, ALU.add))
                step(q, 16, tt(G, F1, one(W1), ALU.mult))
                step(q, 17, tt(F2, F2, one(W2), ALU.mult))
                step(q, 18, tt(G, G, F2, ALU.add))
                step(q, 19, nc.vector.tensor_copy(part(0), gate[:]))
                step(q, 20, tt(gate_rest[:], gate[:], part(0), ALU.subtract))
                step(q, 21, nc.vector.tensor_copy(part(1), gate_rest[:]))
                step(q, 22, tt(gate_rest[:], gate_rest[:], part(1), ALU.subtract))
                step(q, 23, nc.vector.tensor_copy(part(2), gate_rest[:]))

            def expert_slot(q, n):
                if 1 <= n <= 2 * EXPERTS:
                    m = n - 1
                    dve.wait_ge(S["act_done"], nth(q, "act_done", m + 1))
                    dve.wait_ge(S["spread_done"], nth(q, "spread_done", m + 1))
                    if m >= 2:
                        dve.wait_ge(S["down_done"], nth(q, "down_done", m // 2))
                    tt(hidw[:, m % 2, :], hid[:, m % 2, :], bank[6][:], ALU.mult).then_inc(S["weighted"], 1)

            def finish(q):
                dve.wait_ge(S["ffn_turned"], nth(q, "ffn_turned"))
                if later(q):
                    dve.wait_ge(S["y_stored"], nth(before(q), "y_stored"))
                tt(y[:], h2[:], bank[4][:], ALU.add).then_inc(S["out_ready"], 1)

            def iteration(qa, qb):
                on_a, on_b = qa is not None, qb is not None
                slots = iter(range(SLOTS))

                def experts(n=1):
                    for _ in range(n if on_b else 0):
                        expert_slot(qb, next(slots))

                if on_a:
                    move_x(qa)
                if on_b:
                    head_norm(qb)
                    head_out(qb)
                if on_a:
                    centre(qa, h_tm, cent1, st1, "ln1", "htm_ready")
                if on_b:
                    centre(qb, h2, cent2, st2, "ln2", "h2_ready")
                if on_a:
                    variance(qa, sq1, st1, "ln1", LN_EPS)
                if on_b:
                    variance(qb, sq2, st2, "ln2", LN_EPS)
                if on_a:
                    dve.wait_ge(S["ln1_rstd"], nth(qa, "ln1_rstd"))
                    tt(grp(x1_tm[:]), grp(cent1[:]), wide(st1[:, 3, :]), ALU.mult).then_inc(S["ln1_done"], 1)
                if on_b:
                    ln2_scale(qb)
                if on_a:
                    mixes(qa)
                if on_b:
                    ln2_finish(qb)
                if on_a:
                    decay_sums(qa)
                if on_b:
                    top_experts(qb)
                if on_a:
                    prepare(qa)
                if on_b:
                    top_gates(qb)
                if on_a:
                    for c in range(NCH):
                        mask(qa, c)
                experts()
                for lvl in range(LEVELS):
                    if on_a:
                        mask_y(qa, lvl, 0)
                        mask_y(qa, lvl, 1)
                    experts()
                if on_a:
                    move_bonus(qa)
                for c in range(NCH):
                    experts(2 if c == NCH - 1 else 1)
                    if on_a:
                        move_sa(qa, c)
                    experts()
                    if on_a and c < NCH - 1:
                        new_state(qa, c)
                    if c < NCH - 1:
                        experts()
                if on_b:
                    finish(qb)

            dve.wait_ge(c_loaded, n_c)
            tt(wconv[:], wconv[:], filt[:].unsqueeze(2).broadcast_to([P, TAPS, D]), ALU.mult).then_inc(w_built, 1)
            nc.vector.tensor_copy(eye_h[:], eye[:])
            dve.wait_ge(w_zeroed, 1)
            dve.wait_ge(w_loaded, n_w)
            nc.vector.tensor_copy(spread[:], wide(gate_row, P))
            nc.vector.tensor_copy(b_parts[:, 0, :], b_down[:]).then_inc(w_built, 1)
            dve.wait_ge(w_built, 2)
            tt(b_rest[:], b_down[:], b_parts[:, 0, :], ALU.subtract).then_inc(w_built, 1)
            dve.wait_ge(w_built, 3)
            nc.vector.tensor_copy(b_parts[:, 1, :], b_rest[:]).then_inc(w_built, 1)
            dve.wait_ge(w_built, 4)
            tt(b_rest[:], b_rest[:], b_parts[:, 1, :], ALU.subtract).then_inc(w_built, 1)
            dve.wait_ge(w_built, 5)
            nc.vector.tensor_copy(b_parts[:, 2, :], b_rest[:]).then_inc(w_built, 1)
            pipeline(dve, iteration)


_INS = ["x", "L0_tok_filt", "L0_tok_W_k", "L0_tok_b_k", "L0_attn_x_mix", "L0_attn_W_r", "L0_attn_W_k", "L0_attn_W_v",
        "L0_attn_W_o", "L0_attn_A_w", "L0_attn_B_w", "L0_attn_b_w", "L0_attn_A_a", "L0_attn_B_a", "L0_attn_b_a",
        "L0_attn_A_g", "L0_attn_B_g", "L0_attn_k_k", "L0_attn_k_a", "L0_attn_r_k", "L0_attn_gn_w", "L0_attn_gn_b",
        "L0_ffn_gamma", "L0_ffn_beta", "L0_ffn_Wr", "L0_ffn_br", "L0_ffn_W1", "L0_ffn_b1", "L0_ffn_W2", "L0_ffn_b2"]


def kernel(**inputs):
    import concourse.bacc as _bacc
    from concourse.bass_utils import run_bass_kernel_spmd as _run

    nc = _bacc.Bacc("TRN2", target_bir_lowering=False, num_devices=1)
    arrays, args = {}, {}
    for name in _INS:
        a = np.ascontiguousarray(inputs[name])
        arrays[f"in_{name}"] = a
        args[name.replace("L0_", "")] = nc.dram_tensor(f"in_{name}", a.shape, mybir.dt.from_np(a.dtype), kind="ExternalInput").ap()
    consts = []
    for k, a in enumerate(shape_constants()):
        arrays[f"const_{k}"] = a
        consts.append(nc.dram_tensor(f"const_{k}", a.shape, F32, kind="ExternalInput").ap())
    out = nc.dram_tensor("out", (inputs["x"].shape[0], T, D), F32, kind="ExternalOutput").ap()
    audio_tower(nc, args, out, *consts)
    r = _run(nc, [arrays], core_ids=[0])
    return r.results[0]["out"]
```

```python
from contextlib import ExitStack
from itertools import islice

import numpy as np

import concourse.bass as bass
from concourse import mybir

F32 = mybir.dt.float32
F32R = mybir.dt.float32r
I32 = mybir.dt.int32
BF16 = mybir.dt.bfloat16
ALU = mybir.AluOpType
ACT = mybir.ActivationFunctionType
AX_X = mybir.AxisListType.X

P = 128
D = 64
HALF = 64
TAPS = 8
CHUNK = 62
NCH = 4
T = CHUNK * NCH
QUAD = 4
COLS = NCH * P
EXPERTS = 8
HID = 128
LEVELS = 5
DECAY_SCALE = -0.6065306597126334
LN_EPS = 1e-5
GN_EPS = D * 1e-5
HIGH_BITS = -4096


PER = dict(
    x_loaded=16, x_turned=2, xT_ready_v=1, xT_ready_s=1, conv_done=2, h_ready=2, h_turned=1, htm_ready=1,
    ln1_sum=1, ln1_mean=1, ln1_cent=1, ln1_sq=1, ln1_ss=1, ln1_var=1, ln1_rstd=1, ln1_done=1,
    x1_turned=1, x1T_ready=1, delta_ready=3, mixed=6,
    w_proj=2, w_act=2, a_proj=1, a_act=1, g_proj=3, g_act=3, k_proj=1, k_act=1, kk_sq=1, r_proj=1, r_act=1,
    v_proj=1, v_act=1, cum_done=1, cumx_done=1, exps=3, kk_norm=1, kk_max=1, kk_inv=1, kk_bc=1, kk_turned=1,
    res_kept=1, g_kept=1, prep=10, rk_ready=1, bonus_done=1, bonus_ready=1, hats_turned=2, hats_ready=2,
    scores_done=4, masked=16, eye_added=2, xt_first=2, x_first=2, x_first_ready=2,
    y_done=10, y_ready=10, z_done=10, z_ready=10, zt_done=8, zt_ready=8,
    r_done=4, r_ready=4, sa_done=4, sa_ready=4, st_done=3, decayed=2, st_ready=6, o_done=1, o_ready=1,
    gn_sum=1, gn_mean=1, gn_cent=1, gn_sq=1, gn_ss=1, gn_var=1, gn_rstd=1, gn_done=1, bv_ready=1,
    on_turned=1, on_ready=1, bv_turned=1, og_sum=1, og_ready=1, att_done=1, h2_ready=1, h2_kept=1,
    ln2_sum=1, ln2_mean=1, ln2_cent=1, ln2_sq=1, ln2_ss=1, ln2_var=1, ln2_rstd=1, ln2_done=1,
    xn_turned=1, xn_ready=1, xn_high=1, xu_low=2, xu_high=2, router_done=1, top=23, gate_tanh=1, gates_turned=1, gatesT_ready=1,
    up_done=16, act_done=16, spread_done=16, weighted=16, down_done=8, ffn_ready=1, ffn_turned=1,
    out_ready=1, y_stored=64,
)


def shape_constants():
    s, t = np.meshgrid(np.arange(P), np.arange(P), indexing="ij")
    same = s // HALF == t // HALF
    eye = (s == t)
    masks = [same & (s < t), same & (s <= t), eye | (same & (s % 2 == 0) & (t == s + 1))]
    for lvl in range(1, LEVELS + 1):
        size = 2 ** lvl
        masks.append(eye | (same & (s // (2 * size) == t // (2 * size)) & (s // size > t // size)))
    keep = np.ones((P, COLS), np.float32)
    keep[:, ::HALF] = 0.0
    half_ones = np.zeros((P, 2), np.float32)
    half_ones[:HALF, 0] = half_ones[HALF:, 1] = 1.0
    rank = np.tile(np.arange(EXPERTS, 0, -1, dtype=np.float32), (P, 1))
    gate_row = np.zeros((P, 2 * EXPERTS), np.float32)
    for n in range(2 * EXPERTS):
        a, e = n % 2, n // 2
        for part in range(3):
            gate_row[32 * part + 8 * a + e, n] = 1.0
    return dict(eye=eye.astype(np.float32), masks=np.stack(masks, 1).astype(np.float32).reshape(P, -1), keep=keep,
                half_ones=half_ones, rank=rank, minus_half=np.full((P, 8), -0.5, np.float32), gate_row=gate_row)


FIRST = dict(eye=P, wconv=TAPS * D, filt=TAPS, vec=16, minus_half=8)
FRONT = dict(bd=8 * P, w_g1=P, w_g2=D, keep=COLS, half_ones=2)
REST = dict(masks=(3 + LEVELS) * P, rk_col=2, w_router=2 * EXPERTS, router_b=2 * EXPERTS, rank=8, gate_row=2 * EXPERTS,
            b_up=EXPERTS, w_down=EXPERTS * D, b_down=P)


def packed(w):
    def twice(t):
        return np.concatenate([t, t], 0)

    def diagonal(t):
        n, m = t.shape
        out = np.zeros((2 * n, 2 * m), t.dtype)
        out[:n, :m] = out[n:, m:] = t
        return out

    c = shape_constants()
    c["wconv"] = w["tok_W_k"].reshape(TAPS, P, D).transpose(1, 0, 2).reshape(P, -1)
    c["filt"] = w["tok_filt"].T
    vectors = ("tok_b_k", "attn_b_w", "attn_b_a", "attn_k_k", "attn_k_a", "attn_gn_w", "attn_gn_b", "ffn_gamma", "ffn_beta")
    vec = np.concatenate([np.stack([w[n] for n in vectors], 1), w["attn_x_mix"].T], 1)
    c["vec"] = twice(np.concatenate([vec, np.zeros((D, 1), vec.dtype)], 1))
    square = [w["attn_W_r"], w["attn_W_k"], w["attn_W_v"], w["attn_A_a"].T, w["attn_B_a"],
              w["attn_A_w"], w["attn_B_w"], w["attn_W_o"]]
    c["bd"] = np.concatenate([diagonal(m) for m in square], 1)
    c["w_g1"] = twice(w["attn_A_g"])
    c["w_g2"] = w["attn_B_g"]
    c["rk_col"] = diagonal(w["attn_r_k"][:, None])
    c["w_router"] = diagonal(w["ffn_Wr"])
    c["router_b"] = np.tile(w["ffn_br"], (P, 2))
    c["b_up"] = w["ffn_b1"].T
    c["w_down"] = w["ffn_W2"].transpose(1, 0, 2).reshape(HID, -1)
    c["b_down"] = np.zeros((P, P), w["ffn_b2"].dtype)
    for part in range(3):
        c["b_down"][32 * part:32 * part + 16] = diagonal(w["ffn_b2"])
    arrays = {k: np.concatenate([c[n] for n in group], 1) for k, group in (("first", FIRST), ("front", FRONT), ("rest", REST))}
    arrays["up"] = twice(w["ffn_W1"].transpose(1, 0, 2).reshape(D, -1))
    return {k: np.ascontiguousarray(a) for k, a in arrays.items()}


def audio_tower(nc, x, weights, out):
    QUADS = x.shape[0] // QUAD
    SLOTS = 2 * EXPERTS + 2
    FIRST_SLOTS = 11
    AFTER_STATE = (1, 0, 1, 0)
    assert QUADS > 4
    with ExitStack() as ctx:
        def sb(name, *shape, dt=F32):
            return ctx.enter_context(nc.sbuf_tensor(name, [P, *shape], dt))

        S = {n: ctx.enter_context(nc.semaphore(n)) for n in PER}
        first_loaded, w_loaded, zeroed, w_built = (
            ctx.enter_context(nc.semaphore(n)) for n in ("first_loaded", "w_loaded", "zeroed", "w_built"))
        psum = ctx.enter_context(nc.psum_tensor("psum", [P, 8, 512], F32))
        bank = [psum[:, k, :] for k in range(8)]

        first, front, rest = (sb(n, sum(g.values())) for n, g in (("first", FIRST), ("front", FRONT), ("rest", REST)))

        def part(tile, group, name, *shape):
            at = sum(list(group.values())[:list(group).index(name)])
            t = tile[:, at:at + group[name]]
            return t.rearrange("p (a n) -> p a n", a=shape[0]) if shape else t

        eye, filt, vec, minus_half = (part(first, FIRST, n) for n in ("eye", "filt", "vec", "minus_half"))
        wconv = part(first, FIRST, "wconv", TAPS)
        bd = part(front, FRONT, "bd", 8)
        w_g1, w_g2, keep, half_ones = (part(front, FRONT, n) for n in ("w_g1", "w_g2", "keep", "half_ones"))
        masks = part(rest, REST, "masks", 3 + LEVELS)
        rk_col, w_router, router_b, rank, gate_row, b_up, b_down = (
            part(rest, REST, n) for n in ("rk_col", "w_router", "router_b", "rank", "gate_row", "b_up", "b_down"))
        w_down = part(rest, REST, "w_down", EXPERTS)
        W_R, W_K, W_V, W_A1, W_A2, W_W1, W_W2, W_O = range(8)
        (B_CONV, B_W, B_A, K_K, K_A, GN_W, GN_B, GAMMA, BETA) = range(9)
        MIX = 9
        eye_h = sb("eye_h", P, dt=BF16)
        w_parts = sb("w_parts", 2, EXPERTS, HID, dt=F32R)
        b_rest = sb("b_rest", P)
        b_parts = sb("b_parts", 3, P, dt=BF16)
        spread = sb("spread", 2 * EXPERTS, P, dt=BF16)

        xin = sb("xin", 2 * QUAD, P)
        xT = sb("xT", QUAD, 256)
        hT = sb("hT", COLS)
        h_tm, h_res = sb("h_tm", COLS), sb("h_res", COLS)
        cent1, cent2, cent_g = sb("cent1", COLS), sb("cent2", COLS), sb("cent_g", COLS)
        sq1, sq2, sq_g = sb("sq1", COLS), sb("sq2", COLS), sb("sq_g", COLS)
        st1, st2, st_g, st_k = sb("st1", 4, 8), sb("st2", 4, 8), sb("st_g", 4, 8), sb("st_k", 2, 8)
        x1_tm = sb("x1_tm", COLS)
        x1T = sb("x1T", COLS)
        delta = sb("delta", COLS)
        xm = sb("xm", 6, COLS)
        M_R, M_W, M_K, M_V, M_A, M_G = range(6)
        low_w = sb("low_w", COLS)
        w_a = sb("w_a", P)
        sig_w, aT = sb("sig_w", COLS), sb("aT", COLS)
        sig_g = sb("sig_g", 2, COLS)
        gT, g_new, rT, kT, v_tm = sb("gT", COLS), sb("g_new", COLS), sb("rT", COLS), sb("kT", COLS), sb("v_tm", COLS)
        cum, cumx = sb("cum", COLS), sb("cumx", COLS)
        e_in, e_ex, e_neg = sb("e_in", COLS), sb("e_ex", COLS), sb("e_neg", COLS)
        kk2, inv_b, kkn, ka = sb("kk2", COLS), sb("inv_b", COLS), sb("kkn", COLS), sb("ka", COLS)
        k2, t1 = sb("k2", COLS), sb("t1", COLS)
        ar = sb("ar", 2, COLS)
        bt, kt, bh, kh, rk = sb("bt", COLS), sb("kt", COLS), sb("bh", COLS), sb("kh", COLS), sb("rk", COLS)
        bonus = sb("bonus", 8)
        bh_tm, kh_tm = sb("bh_tm", COLS), sb("kh_tm", COLS)
        NT, RB, AK, RK = (sb(n, NCH, 2, P) for n in ("NT", "RB", "AK", "RK"))
        X, XT, Y = (sb(n, NCH, 2, P) for n in ("X", "XT", "Y"))
        r_sb, sa = sb("r_sb", P), sb("sa", P)
        state, state_d = sb("state", 2, P), sb("state_d", 2, P)
        o_tm = sb("o_tm", COLS)
        bv, onT, ogT, xnT = sb("bv", COLS), sb("onT", COLS), sb("ogT", COLS), sb("xnT", COLS)
        h2_new, h2 = sb("h2_new", COLS), sb("h2", COLS)
        xn_h = sb("xn_h", COLS)
        xu = sb("xu", 2, COLS, dt=F32R)
        tops = sb("tops", 13, 8, EXPERTS)
        gate, gate_rest = sb("gate", NCH, 2 * EXPERTS), sb("gate_rest", NCH, 2 * EXPERTS)
        gate_parts = sb("gate_parts", NCH, P, dt=BF16)
        gateT = sb("gateT", COLS, dt=BF16)
        hid, hidw = sb("hid", 2, COLS), sb("hidw", 2, COLS)
        w_up, w_high = (t.rearrange("p a n -> p (a n)").rearrange("p (e h) -> p e h", e=EXPERTS) for t in (hidw, hid))
        ffnT = sb("ffnT", COLS)
        y = sb("y", COLS)

        def fm(t):
            return t.rearrange("p (c b t) -> p c b t", c=NCH, b=2)

        def grp(t, n=8):
            return t.rearrange("p (g d) -> p g d", g=n)

        def wide(t, n=D):
            return t.unsqueeze(2).broadcast_to([P, t.shape[1], n])

        def group(t, g):
            return t[:, 2 * g:2 * g + 2].rearrange("p c a t -> p (c a) t")

        def four(t):
            return t.unsqueeze(1).broadcast_to([P, 4, P])

        dup = [slice(0, 64), slice(64, 128)]

        block = ctx.enter_context(nc.Block())

        def nth(q, name, k=None):
            reg, off = q if isinstance(q, tuple) else (None, q)
            const = off * PER[name] + (PER[name] if k is None else k)
            return const if reg is None else reg * PER[name] + const

        def exists(q):
            return isinstance(q, tuple) or 0 <= q < QUADS

        def later(q):
            return isinstance(q, tuple) or q > 0

        def gate_bank(q, m):
            return 3 if q == QUADS - 1 and m % 2 else 6

        def shifted(q, by):
            return (q[0], q[1] + by) if isinstance(q, tuple) else q + by

        def before(q):
            return shifted(q, -1)

        def pipeline(eng, iteration, late_weights):
            iteration(0, None, None, None)
            late_weights()
            iteration(1, 0, None, None)
            iteration(2, 1, 0, None)
            iteration(3, 2, 1, 0)
            with eng.Fori(3, QUADS - 1) as i:
                iteration((i, 1), (i, 0), (i, -1), (i, -2))
            iteration(None, QUADS - 1, QUADS - 2, QUADS - 3)
            iteration(None, None, QUADS - 1, QUADS - 2)
            iteration(None, None, None, QUADS - 1)

        @block.sync
        def _(sp):
            x_q = x.rearrange("s (h p) f -> p (s h) f", p=P)

            def load_x(q):
                src = x_q[:, bass.ds(q[0] * 8 + 8 * q[1], 8) if isinstance(q, tuple) else slice(8 * q, 8 * q + 8), :]
                sp.dma_start(xin[:], src).then_inc(S["x_loaded"], 16)

            load_x(0)
            sp.dma_start(first[:], weights["first"]).then_inc(first_loaded, 16)
            sp.dma_start(front[:], weights["front"]).then_inc(w_loaded, 16)
            sp.dma_start(rest[:], weights["rest"]).then_inc(w_loaded, 16)
            sp.dma_start(w_up[:], weights["up"].rearrange("p (e h) -> p e h", e=EXPERTS)).then_inc(w_loaded, 16)

            def store(q):
                sp.wait_ge(S["out_ready"], nth(q, "out_ready"))
                yv = y[:].rearrange("p (c a d) -> p c a d", c=NCH, a=2)
                for b in range(2):
                    for a in range(2):
                        s = 2 * a + b
                        row = (bass.ds(q[0] * QUAD + (q[1] * QUAD + s), 1) if isinstance(q, tuple)
                               else slice(QUAD * q + s, QUAD * q + s + 1))
                        sp.dma_start(out[row, :, :].rearrange("s (c t) d -> t (s c) d", c=NCH),
                                     yv[b * HALF:b * HALF + CHUNK, :, a, :]).then_inc(S["y_stored"], 16)

            def load_next(q):
                sp.wait_ge(S["x_turned"], nth(q, "x_turned"))
                load_x(shifted(q, 1))

            for q in range(4):
                load_next(q)
            store(0)
            with sp.Fori(3, QUADS - 2) as i:
                load_next((i, 1))
                store((i, -2))
            for q in range(QUADS - 4, QUADS):
                store(q)
            sp.wait_ge(S["y_stored"], nth(QUADS - 1, "y_stored"))

        @block.gpsimd
        def _(pool):
            for tile in (delta[:], hT[:], state[:], state_d[:], gate_parts[:]):
                last = nc.gpsimd.memset(tile, 0.0)
            last.then_inc(zeroed, 1)
            pool.wait_ge(first_loaded, 16)

            def rsqrt(q, st, src, dst, ready, done):
                pool.wait_ge(S[ready], nth(q, ready))
                nc.gpsimd.tensor_tensor(st[:, dst, :], st[:, src, :], minus_half, ALU.pow).then_inc(S[done], 1)

            def first_inverse(q, g):
                pool.wait_ge(S["masked"], nth(q, "masked", 8 * g + 5))
                nc.gpsimd.tensor_tensor(group(NT, g), group(NT, g), four(eye[:]), ALU.add).then_inc(S["eye_added"], 1)
                pool.wait_ge(S["eye_added"], nth(q, "eye_added", g + 1))
                nc.gpsimd.tensor_tensor(group(XT, g), group(NT, g), four(masks[:, 2, :]), ALU.mult).then_inc(S["xt_first"], 1)

            def iteration(qc, qa, qb, qd):
                on_a, on_b, on_c = qa is not None, qb is not None, qc is not None
                if on_b:
                    rsqrt(qb, st_g, 2, 3, "gn_var", "gn_rstd")
                if on_a:
                    rsqrt(qa, st_k, 0, 1, "kk_max", "kk_inv")
                    first_inverse(qa, 0)
                    first_inverse(qa, 1)
                if on_b:
                    rsqrt(qb, st2, 2, 3, "ln2_var", "ln2_rstd")
                if on_c:
                    rsqrt(qc, st1, 2, 3, "ln1_var", "ln1_rstd")

            def late_weights():
                pool.wait_ge(w_loaded, 48)

            pipeline(pool, iteration, late_weights)

        @block.tensor
        def _(pe):
            mm = nc.tensor.matmul

            def turn(dst, src, done):
                for c in range(NCH):
                    last = nc.tensor.transpose(dst[:, c * P:(c + 1) * P], src[:, c * P:(c + 1) * P], eye[:])
                last.then_inc(S[done], 1)

            def chunk_b(c, b):
                return slice(c * P + b * HALF, c * P + b * HALF + HALF)

            def turn_x(q, h):
                if exists(shifted(q, -3)):
                    pe.wait_ge(S["ffn_ready"], nth(shifted(q, -3), "ffn_ready"))
                pe.wait_ge(S["x_loaded"], nth(q, "x_loaded"))
                for s in range(QUAD):
                    last = nc.tensor.transpose(bank[6 + h][:, s * P:(s + 1) * P], xin[:, 4 * h + s, :], eye[:])
                last.then_inc(S["x_turned"], 1)

            def conv(q, b):
                if b == 0:
                    pe.wait_ge(S["xT_ready_v"], nth(q, "xT_ready_v"))
                    pe.wait_ge(S["xT_ready_s"], nth(q, "xT_ready_s"))
                for f in range(TAPS):
                    for a in range(2):
                        last = mm(bank[6 + b][dup[a], 0:T], wconv[:, f, :], xT[:, 2 * a + b, f:f + T],
                                  start=(f == 0), stop=(f == TAPS - 1))
                last.then_inc(S["conv_done"], 1)

            def turn_h(q):
                pe.wait_ge(S["h_ready"], nth(q, "h_ready"))
                turn(bank[6], hT, "h_turned")

            def turn_x1(q):
                if later(q):
                    pe.wait_ge(S["hats_ready"], nth(before(q), "hats_ready"))
                pe.wait_ge(S["ln1_done"], nth(q, "ln1_done"))
                turn(bank[5], x1_tm, "x1_turned")

            def project(q, m, ready, w, bk, done, free=None):
                if free:
                    pe.wait_ge(S[free], nth(q, free))
                pe.wait_ge(S["mixed"], nth(q, "mixed", ready))
                mm(bank[bk][:], bd[:, w, :], xm[:, m, :], start=True, stop=True).then_inc(S[done], 1)

            def projections_1(q):
                if later(q):
                    pe.wait_ge(S["st_ready"], nth(before(q), "st_ready"))
                    pe.wait_ge(S["o_ready"], nth(before(q), "o_ready"))
                project(q, M_W, 1, W_W1, 2, "w_proj")
                pe.wait_ge(S["mixed"], nth(q, "mixed", 2))
                mm(bank[3][:], w_a[:], xm[:, M_A, :], start=True, stop=True).then_inc(S["a_proj"], 1)
                pe.wait_ge(S["w_act"], nth(q, "w_act", 1))
                mm(bank[2][:], bd[:, W_W2, :], low_w[:], start=True, stop=True).then_inc(S["w_proj"], 1)
                project(q, M_K, 3, W_K, 0, "k_proj")

            def projections_2(q):
                pe.wait_ge(S["w_act"], nth(q, "w_act", 2))
                pe.wait_ge(S["mixed"], nth(q, "mixed", 4))
                mm(bank[2][:], w_g1[dup[0], :], xm[dup[0], M_G, :], start=True, stop=True).then_inc(S["g_proj"], 1)
                pe.wait_ge(S["kk_sq"], nth(q, "kk_sq"))
                for c in range(NCH):
                    last = mm(bank[1][:, 2 * c:2 * c + 2], kk2[:, c * P:(c + 1) * P], half_ones, start=True, stop=True)
                last.then_inc(S["kk_norm"], 1)
                pe.wait_ge(S["a_act"], nth(q, "a_act"))
                mm(bank[3][:], w_g1[dup[1], :], xm[dup[1], M_G, :], start=True, stop=True).then_inc(S["g_proj"], 1)
                project(q, M_R, 5, W_R, 1, "r_proj", free="kk_max")
                pe.wait_ge(S["k_act"], nth(q, "k_act"))
                pe.wait_ge(S["mixed"], nth(q, "mixed", 6))
                for c in range(NCH):
                    last = mm(bank[0][:, c * P:(c + 1) * P], xm[:, M_V, c * P:(c + 1) * P], bd[:, W_V, :],
                              start=True, stop=True)
                last.then_inc(S["v_proj"], 1)

            def projections_3(q):
                pe.wait_ge(S["v_act"], nth(q, "v_act"))
                pe.wait_ge(S["g_act"], nth(q, "g_act", 2))
                for a in range(2):
                    last = mm(bank[0][dup[a], :], w_g2[:], sig_g[:, a, :], start=True, stop=True)
                last.then_inc(S["g_proj"], 1)

            def turn_inverse_norms(q):
                pe.wait_ge(S["r_act"], nth(q, "r_act"))
                pe.wait_ge(S["kk_bc"], nth(q, "kk_bc"))
                turn(bank[1], inv_b, "kk_turned")

            def hat(q, k, src):
                if k > 0:
                    pe.wait_ge(S["hats_ready"], nth(q, "hats_ready", k))
                elif later(q):
                    pe.wait_ge(S["h2_ready"], nth(before(q), "h2_ready"))
                pe.wait_ge(S["prep"], nth(q, "prep", 9 + k))
                turn(bank[5], src, "hats_turned")

            def scores(q, c):
                if c == 0:
                    pe.wait_ge(S["g_act"], nth(q, "g_act"))
                    pe.wait_ge(S["prep"], nth(q, "prep", 8))
                elif c == 1 and later(q):
                    pe.wait_ge(S["og_sum"], nth(before(q), "og_sum"))
                elif c >= 2:
                    pe.wait_ge(S["masked"], nth(q, "masked", 4 * (c - 1)))
                cols = slice(c * P, (c + 1) * P)
                for a in range(2):
                    for key, src in enumerate((bt, kt)):
                        score = bank[2 * (c % 2) + a][:, 256 * key:256 * key + 256].rearrange("p (r t) -> p r t", r=2)
                        if a == 0 and key == 0:
                            mm(score, src[dup[a], cols], ar[dup[a], :, cols], start=True, stop=True)
                            continue
                        for b in range(2):
                            last = mm(score[dup[b], :, dup[b]], src[dup[a], chunk_b(c, b)], ar[dup[a], :, chunk_b(c, b)],
                                      start=True, stop=True)
                last.then_inc(S["scores_done"], 1)

            def x_first(q, g):
                pe.wait_ge(S["xt_first"], nth(q, "xt_first", g + 1))
                pe.wait_ge(S["masked"], nth(q, "masked", 12))
                for u in range(4):
                    last = nc.tensor.transpose(bank[g][:, u * P:(u + 1) * P], XT[:, 2 * g + u // 2, u % 2, :], eye[:])
                last.then_inc(S["x_first"], 1)

            def level_y(q, lvl, g):
                if lvl == 0:
                    pe.wait_ge(S["masked"], nth(q, "masked"))
                    pe.wait_ge(S["x_first_ready"], nth(q, "x_first_ready", g + 1))
                else:
                    pe.wait_ge(S["z_ready"], nth(q, "z_ready", 2 * (lvl - 1) + g + 1))
                for u in range(4):
                    c, a = 2 * g + u // 2, u % 2
                    last = mm(bank[2 + g][:, u * P:(u + 1) * P], NT[:, c, a, :], X[:, c, a, :], start=True, stop=True)
                last.then_inc(S["y_done"], 1)

            def level_z(q, lvl, g):
                pe.wait_ge(S["y_ready"], nth(q, "y_ready", 2 * lvl + g + 1))
                if lvl > 0:
                    pe.wait_ge(S["zt_ready"], nth(q, "zt_ready", 2 * (lvl - 1) + g + 1))
                w, m = (XT, Y) if lvl < LEVELS - 1 else (Y, XT)
                for u in range(4):
                    c, a = 2 * g + u // 2, u % 2
                    last = mm(bank[g][:, u * P:(u + 1) * P], w[:, c, a, :], m[:, c, a, :], start=True, stop=True)
                last.then_inc(S["z_done"], 1)

            def level_t(q, lvl, g):
                pe.wait_ge(S["z_ready"], nth(q, "z_ready", 2 * lvl + g + 1))
                for u in range(4):
                    last = nc.tensor.transpose(bank[g][:, u * P:(u + 1) * P], X[:, 2 * g + u // 2, u % 2, :], eye[:])
                last.then_inc(S["zt_done"], 1)

            def value(c, a):
                return v_tm[:, c * P + a * D:c * P + a * D + D]

            def chunk_r(q, c):
                if c == 0:
                    pe.wait_ge(S["z_ready"], nth(q, "z_ready"))
                else:
                    pe.wait_ge(S["sa_ready"], nth(q, "sa_ready", c))
                    pe.wait_ge(S["st_ready"], nth(q, "st_ready", 2 * c))
                for a in range(2):
                    last = mm(bank[0][:, a * D:a * D + D], AK[:, c, a, :], value(c, a), start=(a == 0),
                              stop=(c == 0), skip_group_check=True)
                if c > 0:
                    for b in range(2):
                        last = mm(bank[0][dup[b], 0:P], ar[:, 0, chunk_b(c, b)], state[:, b, :], start=False, stop=True,
                                  skip_group_check=True)
                last.then_inc(S["r_done"], 1)

            def chunk_sa(q, c):
                pe.wait_ge(S["r_ready"], nth(q, "r_ready", c + 1))
                for a in range(2):
                    last = mm(bank[0][:, P + a * D:P + a * D + D], XT[:, c, a, :], r_sb[:, a * D:a * D + D],
                              start=True, stop=True)
                last.then_inc(S["sa_done"], 1)

            def chunk_bonus(q):
                pe.wait_ge(S["rk_ready"], nth(q, "rk_ready"))
                for c in range(NCH):
                    last = mm(bank[3][:, 2 * c:2 * c + 2], rk[:, c * P:(c + 1) * P], rk_col[:], start=True, stop=True)
                last.then_inc(S["bonus_done"], 1)

            def chunk_o1(q, c):
                if c == 0:
                    pe.wait_ge(S["bonus_ready"], nth(q, "bonus_ready"))
                o0 = c * P
                for a in range(2):
                    mm(bank[1][:, o0 + a * D:o0 + a * D + D], RK[:, c, a, :], value(c, a), start=(a == 0), stop=False,
                       skip_group_check=True)
                if c > 0:
                    for b in range(2):
                        mm(bank[1][dup[b], o0:o0 + P], ar[:, 1, chunk_b(c, b)], state[:, b, :], start=False, stop=False,
                           skip_group_check=True)

            def chunk_o2(q, c):
                pe.wait_ge(S["sa_ready"], nth(q, "sa_ready", c + 1))
                o0 = c * P
                for a in range(2):
                    last = mm(bank[1][:, o0 + a * D:o0 + a * D + D], RB[:, c, a, :], sa[:, a * D:a * D + D],
                              start=False, stop=True, skip_group_check=True)
                if c == NCH - 1:
                    last.then_inc(S["o_done"], 1)

            def chunk_state(q, c):
                for b in range(2):
                    for a in range(2):
                        cols = slice(c * P + a * D, c * P + a * D + D)
                        st = bank[2 + b][dup[a], 0:D]
                        mm(st, bh_tm[dup[b], cols], sa[dup[b], a * D:a * D + D], start=True, stop=False)
                        last = mm(st, kh_tm[dup[b], cols], v_tm[dup[b], cols], start=False, stop=True)
                last.then_inc(S["st_done"], 1)

            def head_norm(q):
                if exists(shifted(q, 1)):
                    pe.wait_ge(S["g_act"], nth(shifted(q, 1), "g_act", 2))
                pe.wait_ge(S["bv_ready"], nth(q, "bv_ready"))
                pe.wait_ge(S["gn_done"], nth(q, "gn_done"))
                turn(bank[2], cent_g, "on_turned")
                turn(bank[3], bv, "bv_turned")

            def out_proj(q):
                if later(q):
                    pe.wait_ge(S["act_done"], nth(before(q), "act_done"))
                pe.wait_ge(S["og_ready"], nth(q, "og_ready"))
                for c in range(NCH):
                    last = mm(bank[5][:, c * P:(c + 1) * P], ogT[:, c * P:(c + 1) * P], bd[:, W_O, :], start=True, stop=True)
                last.then_inc(S["att_done"], 1)

            def turn_xn(q):
                if later(q):
                    pe.wait_ge(S["out_ready"], nth(before(q), "out_ready"))
                pe.wait_ge(S["ln2_done"], nth(q, "ln2_done"))
                turn(bank[4], cent2, "xn_turned")

            def router(q):
                pe.wait_ge(S["xn_ready"], nth(q, "xn_ready"))
                for c in range(NCH):
                    last = mm(bank[4][:, 16 * c:16 * c + 16], xnT[:, c * P:(c + 1) * P], w_router[:], start=True, stop=True)
                last.then_inc(S["router_done"], 1)

            def gates(q):
                if exists(shifted(q, 2)):
                    pe.wait_ge(S["htm_ready"], nth(shifted(q, 2), "htm_ready"))
                pe.wait_ge(S["top"], nth(q, "top"))
                half = bank[6].bitcast(BF16)
                for c in range(NCH):
                    last = nc.tensor.transpose(half[:, c * P:(c + 1) * P], gate_parts[:, c, :], eye_h[:])
                last.then_inc(S["gates_turned"], 1)

            def bias_down(q):
                if exists(shifted(q, 2)):
                    pe.wait_ge(S["h_ready"], nth(shifted(q, 2), "h_ready"))
                    pe.wait_ge(S["x1T_ready"], nth(shifted(q, 2), "x1T_ready"))
                pe.wait_ge(S["gatesT_ready"], nth(q, "gatesT_ready"))
                for part in range(3):
                    mm(bank[7][:], b_parts[:, part, :], gateT[:], start=(part == 0), stop=False, skip_group_check=True)

            def expert_slot(q, n):
                if n < 2 * EXPERTS:
                    e, a = n // 2, n % 2
                    if n >= 2:
                        pe.wait_ge(S["act_done"], nth(q, "act_done", n - 1))
                    else:
                        pe.wait_ge(S["xu_low"], nth(q, "xu_low", n + 1))
                        pe.wait_ge(S["xu_high"], nth(q, "xu_high", n + 1))
                    mm(bank[4 + a][:], w_parts[:, 0, e, :], xu[:, a, :], start=True, stop=False)
                    mm(bank[4 + a][:], w_parts[:, 1, e, :], xu[:, a, :], start=False, stop=True).then_inc(S["up_done"], 1)
                if 1 <= n <= 2 * EXPERTS:
                    taken = n - 2 if q == QUADS - 1 else n - 1
                    if taken > 0:
                        pe.wait_ge(S["weighted"], nth(q, "weighted", taken))
                    mm(bank[gate_bank(q, n - 1)][:], spread[:, n - 1, :], gateT[:], start=True, stop=True).then_inc(S["spread_done"], 1)
                if n % 2 == 1 and n >= 3:
                    e = (n - 3) // 2
                    pe.wait_ge(S["weighted"], nth(q, "weighted", 2 * e + 2))
                    for a in range(2):
                        last = mm(bank[7][dup[a], :], w_down[:, e, :], hidw[:, a, :], start=False, stop=(e == EXPERTS - 1),
                                  skip_group_check=True)
                    last.then_inc(S["down_done"], 1)

            def turn_ffn(q):
                pe.wait_ge(S["ffn_ready"], nth(q, "ffn_ready"))
                turn(bank[4], ffnT, "ffn_turned")

            def iteration(qc, qa, qb, qd):
                on_a, on_b, on_c, on_d = (q is not None for q in (qa, qb, qc, qd))
                first, last = iter(range(FIRST_SLOTS)), iter(range(FIRST_SLOTS, SLOTS))

                def experts(n=1):
                    for slot in islice(first, n if on_b else 0):
                        expert_slot(qb, slot)

                def last_experts(n=1):
                    for slot in islice(last, n if on_d else 0):
                        expert_slot(qd, slot)

                last_experts()
                if on_a:
                    projections_1(qa)
                last_experts()
                if on_a:
                    projections_2(qa)
                    turn_inverse_norms(qa)
                if on_b:
                    head_norm(qb)
                if on_a:
                    projections_3(qa)
                last_experts()
                for c in range(NCH):
                    if on_a:
                        scores(qa, c)
                    if c < NCH - 1:
                        last_experts()
                if on_b:
                    out_proj(qb)
                if on_a:
                    x_first(qa, 0)
                last_experts()
                if on_a:
                    level_y(qa, 0, 0)
                if on_d:
                    turn_ffn(qd)
                if on_a:
                    x_first(qa, 1)
                if on_c:
                    turn_x(qc, 0)
                for lvl in range(LEVELS):
                    if on_a:
                        if lvl > 0:
                            level_y(qa, lvl, 0)
                        level_y(qa, lvl, 1)
                    if lvl == 1 and on_c:
                        conv(qc, 0)
                    if lvl == 1 and on_b:
                        turn_xn(qb)
                    if lvl == 2 and on_c:
                        turn_h(qc)
                    if on_a:
                        level_z(qa, lvl, 0)
                        level_z(qa, lvl, 1)
                    if lvl == 1:
                        if on_b:
                            router(qb)
                        if on_c:
                            conv(qc, 1)
                    if on_a and lvl < LEVELS - 1:
                        level_t(qa, lvl, 0)
                    if lvl == 0 and on_c:
                        turn_x(qc, 1)
                    if on_a and lvl in (2, 3):
                        hat(qa, lvl - 2, (bh, kh)[lvl - 2])
                    if on_a and lvl < LEVELS - 1:
                        level_t(qa, lvl, 1)
                if on_a:
                    chunk_bonus(qa)
                if on_b:
                    gates(qb)
                if on_c:
                    turn_x1(qc)
                experts()
                for c in range(NCH):
                    if on_a:
                        chunk_r(qa, c)
                    if c == 0 and on_b:
                        bias_down(qb)
                    experts()
                    if on_a:
                        chunk_sa(qa, c)
                        chunk_o1(qa, c)
                    experts()
                    if on_a:
                        chunk_o2(qa, c)
                        if c < NCH - 1:
                            chunk_state(qa, c)
                    experts(AFTER_STATE[c])

            def late_weights():
                pe.wait_ge(w_loaded, 48)
                pe.wait_ge(w_built, 9)
                pe.wait_ge(S["h_ready"], nth(0, "h_ready"))
                mm(bank[7][:, 0:P], bd[:, W_A1, :], bd[:, W_A2, :], start=True, stop=True).then_inc(w_built, 1)
                pe.wait_ge(w_built, 11)

            pe.wait_ge(w_built, 1)
            pe.wait_ge(first_loaded, 16)
            pipeline(pe, iteration, late_weights)

        @block.scalar
        def _(act):
            copy, activation = nc.scalar.copy, nc.scalar.activation

            def v(k):
                return vec[:, k:k + 1]

            def square(q, dst, src, name):
                act.wait_ge(S[name + "_cent"], nth(q, name + "_cent"))
                activation(dst[:], src[:], ACT.Square).then_inc(S[name + "_sq"], 1)

            def move_x(q):
                act.wait_ge(S["x_turned"], nth(q, "x_turned", 2))
                copy(xT[:, 2:4, :].rearrange("p s t -> p (s t)"), bank[7][:]).then_inc(S["xT_ready_s"], 1)

            def tokens(q, b):
                act.wait_ge(S["conv_done"], nth(q, "conv_done", b + 1))
                activation(fm(hT[:])[:, :, b, 0:CHUNK], bank[6 + b][:, 0:T].rearrange("p (c t) -> p c t", c=NCH),
                           ACT.Relu, bias=v(B_CONV)).then_inc(S["h_ready"], 1)

            def move_h(q):
                if later(q):
                    act.wait_ge(S["res_kept"], nth(before(q), "res_kept"))
                act.wait_ge(S["h_turned"], nth(q, "h_turned"))
                copy(h_tm[:], bank[6][:]).then_inc(S["htm_ready"], 1)

            def move_x1(q):
                act.wait_ge(S["x1_turned"], nth(q, "x1_turned"))
                copy(x1T[:], bank[5][:]).then_inc(S["x1T_ready"], 1)

            def projected_1(q):
                act.wait_ge(S["w_proj"], nth(q, "w_proj", 1))
                activation(low_w[:], bank[2][:], ACT.Tanh).then_inc(S["w_act"], 1)

            def projected_2(q):
                act.wait_ge(S["w_proj"], nth(q, "w_proj", 2))
                activation(sig_w[:], bank[2][:], ACT.Sigmoid, bias=v(B_W)).then_inc(S["w_act"], 1)
                act.wait_ge(S["k_proj"], nth(q, "k_proj"))
                activation(kk2[:], bank[0][:], ACT.Square, scale=v(K_K)).then_inc(S["kk_sq"], 1)
                act.wait_ge(S["a_proj"], nth(q, "a_proj"))
                activation(aT[:], bank[3][:], ACT.Sigmoid, bias=v(B_A)).then_inc(S["a_act"], 1)
                copy(kT[:], bank[0][:]).then_inc(S["k_act"], 1)
                for a in range(2):
                    act.wait_ge(S["g_proj"], nth(q, "g_proj", a + 1))
                    activation(sig_g[:, a, :], bank[2 + a][:], ACT.Sigmoid).then_inc(S["g_act"], 1)
                act.wait_ge(S["r_proj"], nth(q, "r_proj"))
                copy(rT[:], bank[1][:]).then_inc(S["r_act"], 1)

            def projected_v(q):
                act.wait_ge(S["v_proj"], nth(q, "v_proj"))
                if later(q):
                    act.wait_ge(S["bv_ready"], nth(before(q), "bv_ready"))
                copy(v_tm[:], bank[0][:]).then_inc(S["v_act"], 1)

            def move_g(q):
                act.wait_ge(S["g_proj"], nth(q, "g_proj", 3))
                copy(g_new[:], bank[0][:]).then_inc(S["g_act"], 1)

            def keep_g(q):
                if later(q):
                    act.wait_ge(S["og_ready"], nth(before(q), "og_ready"))
                act.wait_ge(S["g_act"], nth(q, "g_act"))
                copy(gT[:], g_new[:]).then_inc(S["g_kept"], 1)

            def decays(q):
                act.wait_ge(S["cum_done"], nth(q, "cum_done"))
                activation(e_neg[:], cum[:], ACT.Exp, scale=-DECAY_SCALE).then_inc(S["exps"], 1)
                projected_v(q)
                act.wait_ge(S["cumx_done"], nth(q, "cumx_done"))
                activation(e_ex[:], cumx[:], ACT.Exp, scale=DECAY_SCALE).then_inc(S["exps"], 1)
                activation(e_in[:], cum[:], ACT.Exp, scale=DECAY_SCALE).then_inc(S["exps"], 1)

            def move_hat(q, k, dst):
                act.wait_ge(S["hats_turned"], nth(q, "hats_turned", k + 1))
                copy(dst[:], bank[5][:]).then_inc(S["hats_ready"], 1)

            def move_first(q, g):
                act.wait_ge(S["x_first"], nth(q, "x_first", g + 1))
                copy(group(X, g), grp(bank[g][:], 4)).then_inc(S["x_first_ready"], 1)

            def move_z(q, lvl, g):
                act.wait_ge(S["z_done"], nth(q, "z_done", 2 * lvl + g + 1))
                copy(group(X if lvl < LEVELS - 1 else XT, g), grp(bank[g][:], 4)).then_inc(S["z_ready"], 1)

            def move_t(q, lvl, g):
                act.wait_ge(S["zt_done"], nth(q, "zt_done", 2 * lvl + g + 1))
                copy(group(XT, g), grp(bank[g][:], 4)).then_inc(S["zt_ready"], 1)

            def move_r(q, c):
                act.wait_ge(S["r_done"], nth(q, "r_done", c + 1))
                copy(r_sb[:], bank[0][:, 0:P]).then_inc(S["r_ready"], 1)

            def move_o(q):
                act.wait_ge(S["o_done"], nth(q, "o_done"))
                copy(o_tm[:], bank[1][:]).then_inc(S["o_ready"], 1)

            def head_affine(q):
                act.wait_ge(S["on_turned"], nth(q, "on_turned"))
                activation(onT[:], bank[2][:], ACT.Identity, scale=v(GN_W), bias=v(GN_B)).then_inc(S["on_ready"], 1)

            def ffn_affine(q):
                act.wait_ge(S["xn_turned"], nth(q, "xn_turned"))
                activation(xnT[:], bank[4][:], ACT.Identity, scale=v(GAMMA), bias=v(BETA)).then_inc(S["xn_ready"], 1)

            def high_rows(q):
                act.wait_ge(S["xn_high"], nth(q, "xn_high"))
                for a in range(2):
                    copy(xu[dup[a], a, :], xn_h[dup[a], :]).then_inc(S["xu_high"], 1)

            def gate_tanh(q):
                act.wait_ge(S["top"], nth(q, "top", 13))
                activation(tops[:, 6, :, 0], tops[:, 5, :, 0], ACT.Tanh, scale=0.5).then_inc(S["gate_tanh"], 1)

            def move_gates(q):
                act.wait_ge(S["gates_turned"], nth(q, "gates_turned"))
                copy(gateT[:], bank[6].bitcast(BF16)[:, 0:COLS]).then_inc(S["gatesT_ready"], 1)

            def expert_slot(q, n):
                if n < 2 * EXPERTS:
                    e, a = n // 2, n % 2
                    act.wait_ge(S["up_done"], nth(q, "up_done", n + 1))
                    if n >= 2:
                        act.wait_ge(S["weighted"], nth(q, "weighted", n - 1))
                    activation(hid[:, a, :], bank[4 + a][:], ACT.Gelu, bias=b_up[:, e:e + 1]).then_inc(S["act_done"], 1)

            def move_ffn(q):
                act.wait_ge(S["down_done"], nth(q, "down_done"))
                copy(ffnT[:], bank[7][:]).then_inc(S["ffn_ready"], 1)

            def iteration(qc, qa, qb, qd):
                on_a, on_b, on_c, on_d = (q is not None for q in (qa, qb, qc, qd))
                first, last = iter(range(FIRST_SLOTS)), iter(range(FIRST_SLOTS, SLOTS))

                def experts(n=1):
                    for slot in islice(first, n if on_b else 0):
                        expert_slot(qb, slot)

                def last_experts(n=1):
                    for slot in islice(last, n if on_d else 0):
                        expert_slot(qd, slot)

                last_experts()
                if on_a:
                    projected_1(qa)
                if on_b:
                    square(qb, sq_g, cent_g, "gn")
                if on_a:
                    projected_2(qa)
                    decays(qa)
                    move_g(qa)
                if on_b:
                    head_affine(qb)
                last_experts(4)
                if on_a:
                    keep_g(qa)
                if on_a:
                    move_first(qa, 0)
                if on_d:
                    move_ffn(qd)
                if on_a:
                    move_first(qa, 1)
                for lvl in range(LEVELS):
                    if lvl == 1:
                        if on_b:
                            square(qb, sq2, cent2, "ln2")
                        if on_c:
                            tokens(qc, 0)
                        if on_b:
                            ffn_affine(qb)
                    if lvl == 2 and on_c:
                        tokens(qc, 1)
                        move_h(qc)
                    if on_a:
                        move_z(qa, lvl, 0)
                        move_z(qa, lvl, 1)
                    if lvl == 1 and on_b:
                        gate_tanh(qb)
                    if lvl == 2:
                        if on_b:
                            high_rows(qb)
                        if on_c:
                            square(qc, sq1, cent1, "ln1")
                    if on_a and lvl < LEVELS - 1:
                        move_t(qa, lvl, 0)
                    if lvl == 0 and on_c:
                        move_x(qc)
                    if lvl in (2, 3) and on_a:
                        move_hat(qa, lvl - 2, (bh_tm, kh_tm)[lvl - 2])
                    if on_a and lvl < LEVELS - 1:
                        move_t(qa, lvl, 1)
                if on_b:
                    move_gates(qb)
                if on_c:
                    move_x1(qc)
                experts()
                for c in range(NCH):
                    if on_a:
                        move_r(qa, c)
                    experts(2 + AFTER_STATE[c])
                if on_a:
                    move_o(qa)

            def late_weights():
                act.wait_ge(w_loaded, 48)
                act.wait_ge(w_built, 10)
                copy(w_a[:], bank[7][:, 0:P]).then_inc(w_built, 1)

            act.wait_ge(first_loaded, 16)
            act.wait_ge(zeroed, 1)
            pipeline(act, iteration, late_weights)

        @block.vector
        def _(dve):
            tt, ts, stt = nc.vector.tensor_tensor, nc.vector.tensor_scalar, nc.vector.scalar_tensor_tensor

            def v(k):
                return vec[:, k:k + 1]

            def centre(q, src, cent, st, name, ready):
                dve.wait_ge(S[ready], nth(q, ready))
                nc.vector.reduce_sum(st[:, 0, :], grp(src[:]), AX_X).then_inc(S[name + "_sum"], 1)
                dve.wait_ge(S[name + "_sum"], nth(q, name + "_sum"))
                ts(st[:, 1, :], st[:, 0, :], -1.0 / D, None, ALU.mult).then_inc(S[name + "_mean"], 1)
                dve.wait_ge(S[name + "_mean"], nth(q, name + "_mean"))
                tt(grp(cent[:]), grp(src[:]), wide(st[:, 1, :]), ALU.add).then_inc(S[name + "_cent"], 1)

            def variance(q, sq, st, name, eps, scale=1.0):
                dve.wait_ge(S[name + "_sq"], nth(q, name + "_sq"))
                nc.vector.reduce_sum(st[:, 0, :], grp(sq[:]), AX_X).then_inc(S[name + "_ss"], 1)
                dve.wait_ge(S[name + "_ss"], nth(q, name + "_ss"))
                ts(st[:, 2, :], st[:, 0, :], scale / D, eps, ALU.mult, ALU.add).then_inc(S[name + "_var"], 1)

            def move_x(q):
                dve.wait_ge(S["x_turned"], nth(q, "x_turned", 1))
                nc.vector.tensor_copy(xT[:, 0:2, :].rearrange("p s t -> p (s t)"), bank[6][:]).then_inc(S["xT_ready_v"], 1)

            def normalise(q):
                dve.wait_ge(S["ln1_rstd"], nth(q, "ln1_rstd"))
                tt(grp(x1_tm[:]), grp(cent1[:]), wide(st1[:, 3, :]), ALU.mult).then_inc(S["ln1_done"], 1)

            def token_steps(q):
                dve.wait_ge(S["x1T_ready"], nth(q, "x1T_ready"))
                xv, dv = fm(x1T[:]), fm(delta[:])
                tt(dv[:, :, :, 1:CHUNK], xv[:, :, :, 0:CHUNK - 1], xv[:, :, :, 1:CHUNK], ALU.subtract).then_inc(S["delta_ready"], 1)
                tt(dv[:, 1:NCH, :, 0], xv[:, 0:NCH - 1, :, CHUNK - 1], xv[:, 1:NCH, :, 0], ALU.subtract).then_inc(S["delta_ready"], 1)
                ts(dv[:, 0, :, 0], xv[:, 0, :, 0], -1.0, None, ALU.mult).then_inc(S["delta_ready"], 1)
                dve.wait_ge(S["delta_ready"], nth(q, "delta_ready"))

            def mix(q, m):
                stt(xm[:, m, :], delta[:], v(MIX + m), x1T[:], ALU.mult, ALU.add).then_inc(S["mixed"], 1)

            def key_norms(q):
                dve.wait_ge(S["kk_norm"], nth(q, "kk_norm"))
                ts(st_k[:, 0, :], bank[1][:, 0:8], 1e-24, None, ALU.max).then_inc(S["kk_max"], 1)

            def decay_sums(q):
                dve.wait_ge(S["w_act"], nth(q, "w_act", 2))
                nc.vector.tensor_tensor_scan(cum[:], keep[:], sig_w[:], 0.0, ALU.mult, ALU.add).then_inc(S["cum_done"], 1)
                dve.wait_ge(S["cum_done"], nth(q, "cum_done"))
                tt(cumx[:], cum[:], sig_w[:], ALU.subtract).then_inc(S["cumx_done"], 1)

            def spread_inverse_norms(q):
                dve.wait_ge(S["kk_inv"], nth(q, "kk_inv"))
                nc.vector.tensor_copy(grp(inv_b[:]), wide(st_k[:, 1, :])).then_inc(S["kk_bc"], 1)

            def prepare_1(q):
                dve.wait_ge(S["a_act"], nth(q, "a_act"))
                ts(t1[:], aT[:], 1.0, v(K_A), ALU.subtract, ALU.mult).then_inc(S["prep"], 1)
                dve.wait_ge(S["prep"], nth(q, "prep", 1))
                dve.wait_ge(S["k_act"], nth(q, "k_act"))
                stt(k2[:], t1[:], 1.0, kT[:], ALU.add, ALU.mult).then_inc(S["prep"], 1)

            def removal_keys(q):
                dve.wait_ge(S["kk_turned"], nth(q, "kk_turned"))
                stt(kkn[:], kT[:], v(K_K), bank[1][:], ALU.mult, ALU.mult).then_inc(S["prep"], 1)
                dve.wait_ge(S["prep"], nth(q, "prep", 3))
                tt(ka[:], kkn[:], aT[:], ALU.mult).then_inc(S["prep"], 1)

            def prepare_2(q):
                dve.wait_ge(S["exps"], nth(q, "exps", 1))
                tt(kt[:], k2[:], e_neg[:], ALU.mult).then_inc(S["prep"], 1)
                dve.wait_ge(S["prep"], nth(q, "prep", 4))
                tt(bt[:], ka[:], e_neg[:], ALU.mult).then_inc(S["prep"], 1)
                dve.wait_ge(S["exps"], nth(q, "exps", 2))
                stt(ar[:, 0, :], kkn[:], -1.0, e_ex[:], ALU.mult, ALU.mult).then_inc(S["prep"], 1)
                dve.wait_ge(S["r_act"], nth(q, "r_act"))
                dve.wait_ge(S["exps"], nth(q, "exps", 3))
                tt(ar[:, 1, :], rT[:], e_in[:], ALU.mult).then_inc(S["prep"], 1)

            def prepare_hats(q):
                dve.wait_ge(S["prep"], nth(q, "prep", 6))
                last_decay = fm(e_in[:])[:, :, :, CHUNK - 1].rearrange("p c b -> p (c b)")
                tt(grp(bh[:]), grp(bt[:]), wide(last_decay), ALU.mult).then_inc(S["prep"], 1)
                tt(grp(kh[:]), grp(kt[:]), wide(last_decay), ALU.mult).then_inc(S["prep"], 1)
                tt(rk[:], rT[:], k2[:], ALU.mult).then_inc(S["rk_ready"], 1)

            def mask(q, c):
                dve.wait_ge(S["scores_done"], nth(q, "scores_done", c + 1))
                both = psum[:, 2 * (c % 2):2 * (c % 2) + 2, :].rearrange("p a (k r t) -> p a k r t", k=2, r=2)
                for key, r, dst in ((0, 0, NT), (0, 1, RB), (1, 0, AK), (1, 1, RK)):
                    tt(dst[:, c, :, :], both[:, :, key, r, :], masks[:, r, :].unsqueeze(1).broadcast_to([P, 2, P]),
                       ALU.mult).then_inc(S["masked"], 1)

            def mask_y(q, lvl, g):
                dve.wait_ge(S["y_done"], nth(q, "y_done", 2 * lvl + g + 1))
                tt(group(Y, g), grp(bank[2 + g][:], 4), four(masks[:, 3 + lvl, :]), ALU.mult).then_inc(S["y_ready"], 1)

            def move_bonus(q):
                dve.wait_ge(S["bonus_done"], nth(q, "bonus_done"))
                nc.vector.tensor_copy(bonus[:], bank[3][:, 0:8]).then_inc(S["bonus_ready"], 1)

            def move_sa(q, c):
                dve.wait_ge(S["sa_done"], nth(q, "sa_done", c + 1))
                nc.vector.tensor_copy(sa[:], bank[0][:, P:2 * P]).then_inc(S["sa_ready"], 1)

            def new_state(q, c):
                dve.wait_ge(S["st_done"], nth(q, "st_done", c + 1))
                if c > 0:
                    dve.wait_ge(S["decayed"], nth(q, "decayed", c))
                for a in range(2):
                    new = psum[dup[a], 2:4, 0:D]
                    if c == 0:
                        nc.vector.tensor_copy(state[dup[a], :, dup[a]], new).then_inc(S["st_ready"], 1)
                    else:
                        tt(state[dup[a], :, dup[a]], state_d[dup[a], :, dup[a]], new, ALU.add).then_inc(S["st_ready"], 1)
                if c < NCH - 2:
                    dve.wait_ge(S["st_ready"], nth(q, "st_ready", 2 * c + 2))
                    tt(state_d[:], state[:], wide(fm(e_in[:])[:, c + 1, :, CHUNK - 1], P), ALU.mult).then_inc(S["decayed"], 1)

            def head_centre(q):
                centre(q, o_tm, cent_g, st_g, "gn", "o_ready")

            def head_bonus(q):
                tt(grp(bv[:]), grp(v_tm[:]), wide(bonus[:]), ALU.mult).then_inc(S["bv_ready"], 1)

            def head_finish(q):
                dve.wait_ge(S["gn_rstd"], nth(q, "gn_rstd"))
                tt(grp(cent_g[:]), grp(cent_g[:]), wide(st_g[:, 3, :]), ALU.mult).then_inc(S["gn_done"], 1)

            def head_out(q):
                dve.wait_ge(S["bv_turned"], nth(q, "bv_turned"))
                dve.wait_ge(S["on_ready"], nth(q, "on_ready"))
                tt(onT[:], onT[:], bank[3][:], ALU.add).then_inc(S["og_sum"], 1)
                dve.wait_ge(S["og_sum"], nth(q, "og_sum"))
                dve.wait_ge(S["g_kept"], nth(q, "g_kept"))
                tt(ogT[:], onT[:], gT[:], ALU.mult).then_inc(S["og_ready"], 1)

            def add_residual(q):
                dve.wait_ge(S["att_done"], nth(q, "att_done"))
                dve.wait_ge(S["res_kept"], nth(q, "res_kept"))
                tt(h2_new[:], h_res[:], bank[5][:], ALU.add).then_inc(S["h2_ready"], 1)

            def keep_h2(q):
                dve.wait_ge(S["h2_ready"], nth(q, "h2_ready"))
                if later(q):
                    dve.wait_ge(S["out_ready"], nth(before(q), "out_ready"))
                nc.vector.tensor_copy(h2[:], h2_new[:]).then_inc(S["h2_kept"], 1)

            def keep_residual(q):
                if later(q):
                    dve.wait_ge(S["h2_ready"], nth(before(q), "h2_ready"))
                dve.wait_ge(S["htm_ready"], nth(q, "htm_ready"))
                nc.vector.tensor_copy(h_res[:], h_tm[:]).then_inc(S["res_kept"], 1)

            def ln2_finish(q):
                dve.wait_ge(S["ln2_rstd"], nth(q, "ln2_rstd"))
                tt(grp(cent2[:]), grp(cent2[:]), wide(st2[:, 3, :]), ALU.mult).then_inc(S["ln2_done"], 1)

            def split_rows(q):
                dve.wait_ge(S["xn_ready"], nth(q, "xn_ready"))
                ts(xn_h.bitcast(I32)[:], xnT.bitcast(I32)[:], HIGH_BITS, None, ALU.bitwise_and).then_inc(S["xn_high"], 1)
                dve.wait_ge(S["xn_high"], nth(q, "xn_high"))
                for a in range(2):
                    tt(xu[dup[1 - a], a, :], xnT[dup[a], :], xn_h[dup[a], :], ALU.subtract).then_inc(S["xu_low"], 1)

            L, EQ, EQ2, T1, T2, DIFF, TH, F1, F2, MX, L2, W1, W2 = (tops[:, k] for k in range(13))
            G = gate[:].rearrange("p c (a e) -> p (c a) e", a=2)
            ranks = rank.unsqueeze(1).broadcast_to([P, 8, EXPERTS])

            def one(t):
                return t[:, :, 0:1].broadcast_to([P, 8, EXPERTS])

            def step(q, k, instruction):
                instruction.then_inc(S["top"], 1)
                dve.wait_ge(S["top"], nth(q, "top", k))

            def top_experts(q):
                dve.wait_ge(S["router_done"], nth(q, "router_done"))
                step(q, 1, tt(L.rearrange("p (c a) e -> p c (a e)", a=2),
                             bank[4][:, 0:64].rearrange("p (c e) -> p c e", c=NCH),
                             router_b[:].unsqueeze(1).broadcast_to([P, NCH, 16]), ALU.add))
                step(q, 2, nc.vector.tensor_reduce(T1[:, :, 0], L, AX_X, ALU.max))
                step(q, 3, tt(EQ, L, one(T1), ALU.is_equal))
                step(q, 4, tt(EQ, EQ, ranks, ALU.mult))
                step(q, 5, nc.vector.tensor_reduce(MX[:, :, 0], EQ, AX_X, ALU.max))
                step(q, 6, tt(F1, EQ, one(MX), ALU.is_equal))
                step(q, 7, stt(L2, F1, -3e38, L, ALU.mult, ALU.add))
                step(q, 8, nc.vector.tensor_reduce(T2[:, :, 0], L2, AX_X, ALU.max))
                step(q, 9, tt(EQ2, L2, one(T2), ALU.is_equal))
                step(q, 10, tt(EQ2, EQ2, ranks, ALU.mult))
                step(q, 11, nc.vector.tensor_reduce(MX[:, :, 0], EQ2, AX_X, ALU.max))
                step(q, 12, tt(F2, EQ2, one(MX), ALU.is_equal))
                step(q, 13, tt(DIFF[:, :, 0], T2[:, :, 0], T1[:, :, 0], ALU.subtract))

            def top_gates(q):
                def part(k):
                    return gate_parts[:, :, 32 * k:32 * k + 16]

                dve.wait_ge(S["gate_tanh"], nth(q, "gate_tanh"))
                step(q, 14, ts(W1[:, :, 0], TH[:, :, 0], -0.5, 0.5, ALU.mult, ALU.add))
                step(q, 15, ts(W2[:, :, 0], TH[:, :, 0], 0.5, 0.5, ALU.mult, ALU.add))
                step(q, 16, tt(G, F1, one(W1), ALU.mult))
                step(q, 17, tt(F2, F2, one(W2), ALU.mult))
                step(q, 18, tt(G, G, F2, ALU.add))
                step(q, 19, nc.vector.tensor_copy(part(0), gate[:]))
                step(q, 20, tt(gate_rest[:], gate[:], part(0), ALU.subtract))
                step(q, 21, nc.vector.tensor_copy(part(1), gate_rest[:]))
                step(q, 22, tt(gate_rest[:], gate_rest[:], part(1), ALU.subtract))
                step(q, 23, nc.vector.tensor_copy(part(2), gate_rest[:]))

            def expert_slot(q, n):
                if 1 <= n <= 2 * EXPERTS:
                    m = n - 1
                    dve.wait_ge(S["act_done"], nth(q, "act_done", m + 1))
                    dve.wait_ge(S["spread_done"], nth(q, "spread_done", m + 1))
                    if m >= 2:
                        dve.wait_ge(S["down_done"], nth(q, "down_done", m // 2))
                    tt(hidw[:, m % 2, :], hid[:, m % 2, :], bank[gate_bank(q, m)][:], ALU.mult).then_inc(S["weighted"], 1)

            def finish(q):
                dve.wait_ge(S["ffn_turned"], nth(q, "ffn_turned"))
                if later(q):
                    dve.wait_ge(S["y_stored"], nth(before(q), "y_stored"))
                dve.wait_ge(S["h2_kept"], nth(q, "h2_kept"))
                tt(y[:], h2[:], bank[4][:], ALU.add).then_inc(S["out_ready"], 1)

            def build_weights():
                nc.vector.tensor_copy(eye_h[:], eye[:])
                dve.wait_ge(w_loaded, 48)
                nc.vector.tensor_copy(spread[:], wide(gate_row, P))
                ts(w_high.bitcast(I32)[:], w_up.bitcast(I32)[:], HIGH_BITS, None, ALU.bitwise_and).then_inc(w_built, 1)
                dve.wait_ge(w_built, 2)
                nc.vector.tensor_copy(w_parts[:, 0], w_high[:]).then_inc(w_built, 1)
                tt(w_parts[:, 1], w_up[:], w_high[:], ALU.subtract).then_inc(w_built, 1)
                nc.vector.tensor_copy(b_parts[:, 0, :], b_down[:]).then_inc(w_built, 1)
                dve.wait_ge(w_built, 5)
                tt(b_rest[:], b_down[:], b_parts[:, 0, :], ALU.subtract).then_inc(w_built, 1)
                dve.wait_ge(w_built, 6)
                nc.vector.tensor_copy(b_parts[:, 1, :], b_rest[:]).then_inc(w_built, 1)
                dve.wait_ge(w_built, 7)
                tt(b_rest[:], b_rest[:], b_parts[:, 1, :], ALU.subtract).then_inc(w_built, 1)
                dve.wait_ge(w_built, 8)
                nc.vector.tensor_copy(b_parts[:, 2, :], b_rest[:]).then_inc(w_built, 1)

            def iteration(qc, qa, qb, qd):
                on_a, on_b, on_c, on_d = (q is not None for q in (qa, qb, qc, qd))
                first, last = iter(range(FIRST_SLOTS)), iter(range(FIRST_SLOTS, SLOTS))
                mixes = iter((M_W, M_A, M_K, M_G))

                def experts(n=1):
                    for slot in islice(first, n if on_b else 0):
                        expert_slot(qb, slot)

                def last_experts(n=1):
                    for slot in islice(last, n if on_d else 0):
                        expert_slot(qd, slot)

                if on_b:
                    head_centre(qb)
                last_experts()
                if on_b:
                    head_bonus(qb)
                if on_a:
                    mix(qa, M_R)
                if on_b:
                    variance(qb, sq_g, st_g, "gn", GN_EPS)
                if on_a:
                    decay_sums(qa)
                    mix(qa, M_V)
                if on_a:
                    key_norms(qa)
                last_experts()
                if on_a:
                    prepare_1(qa)
                    spread_inverse_norms(qa)
                if on_b:
                    head_finish(qb)
                if on_a:
                    removal_keys(qa)
                    prepare_2(qa)
                if on_b:
                    head_out(qb)
                last_experts()
                for c in range(NCH):
                    if on_a:
                        mask(qa, c)
                    last_experts()
                if on_a:
                    prepare_hats(qa)
                if on_b:
                    add_residual(qb)
                if on_a:
                    keep_residual(qa)
                for lvl in range(LEVELS):
                    if on_a:
                        mask_y(qa, lvl, 0)
                        mask_y(qa, lvl, 1)
                    if lvl == 0:
                        if on_b:
                            centre(qb, h2_new, cent2, st2, "ln2", "h2_ready")
                        if on_c:
                            move_x(qc)
                        if on_d:
                            finish(qd)
                        if qc == 0:
                            build_weights()
                        if on_b:
                            keep_h2(qb)
                            variance(qb, sq2, st2, "ln2", LN_EPS ** 2, 1.0 + LN_EPS)
                    if lvl == 1:
                        if on_b:
                            ln2_finish(qb)
                            top_experts(qb)
                            split_rows(qb)
                    if lvl == 2:
                        if on_c:
                            centre(qc, h_tm, cent1, st1, "ln1", "htm_ready")
                    if lvl == 3:
                        if on_c:
                            variance(qc, sq1, st1, "ln1", LN_EPS)
                        if on_b:
                            top_gates(qb)
                    if lvl == 4 and on_c:
                        normalise(qc)
                if on_a:
                    move_bonus(qa)
                experts()
                if on_c and not on_a:
                    token_steps(qc)
                for c in range(NCH):
                    experts()
                    if on_a:
                        move_sa(qa, c)
                    if on_c and on_a and c == 0:
                        token_steps(qc)
                    experts()
                    if on_a and c < NCH - 1:
                        new_state(qa, c)
                    if on_c:
                        mix(qc, next(mixes))
                    experts(AFTER_STATE[c])

            dve.wait_ge(first_loaded, 16)
            tt(wconv[:], wconv[:], filt[:].unsqueeze(2).broadcast_to([P, TAPS, D]), ALU.mult).then_inc(w_built, 1)
            dve.wait_ge(zeroed, 1)
            pipeline(dve, iteration, lambda: None)


def kernel(**inputs):
    import concourse.bacc as _bacc
    from concourse.bass_utils import run_bass_kernel_spmd as _run

    nc = _bacc.Bacc("TRN2", target_bir_lowering=False, num_devices=1)
    arrays = packed({n[len("L0_"):]: np.asarray(a) for n, a in inputs.items() if n != "x"})
    arrays["x"] = np.ascontiguousarray(inputs["x"])
    aps = {n: nc.dram_tensor(f"in_{n}", a.shape, mybir.dt.from_np(a.dtype), kind="ExternalInput").ap()
           for n, a in arrays.items()}
    out = nc.dram_tensor("out", (inputs["x"].shape[0], T, D), F32, kind="ExternalOutput").ap()
    audio_tower(nc, aps.pop("x"), aps, out)
    arrays = {f"in_{n}": a for n, a in arrays.items()}
    r = _run(nc, [arrays], core_ids=[0])
    return r.results[0]["out"]
```
